# Optimizing a Trainium2 kernel written in Bass

```python
import numpy as np
import jax
import jax.numpy as jnp

def _softmax(x, axis=-1):
    return jax.nn.softmax(x, axis=axis)

def _gelu(x):
    return jax.nn.gelu(x, approximate=True)

def _silu(x):
    return jax.nn.silu(x)

def _sigmoid(x):
    return jax.nn.sigmoid(x)

def _layernorm(x, axis=-1, eps=1e-05):
    m = jnp.mean(x, axis=axis, keepdims=True)
    v = jnp.var(x, axis=axis, keepdims=True)
    return (x - m) / jnp.sqrt(v + eps)

def _scatter_add(tgt, idx, src, axis=0):
    return tgt.at[idx].add(src)

def _segment_sum(src, seg, n):
    return jax.ops.segment_sum(src, seg, n)
kernel_name = 'mk_gnn_resnorm_d2_gnn_r8_e0ad84'

def setup_inputs(seed: int=0):
    np.random.seed(seed)
    _w = jnp.asarray

    def _rec_inputs():
        import jax
        import jax.numpy as jnp
        _gk = jax.random.key(seed)
        x = -0.000202 + 1 * jax.random.normal(jax.random.fold_in(_gk, 1), (12500, 128), jnp.float32)
        src = jax.random.randint(jax.random.fold_in(_gk, 2), (200000,), 0, 12500, jnp.int32)
        dst = jax.random.randint(jax.random.fold_in(_gk, 3), (200000,), 0, 12500, jnp.int32)
        _o = jnp.argsort(dst, stable=True)
        src = src[_o]
        dst = dst[_o]
        return (x, src, dst)
    x, src, dst = _rec_inputs()

    def _L0_gnn_setup():
        import jax, jax.numpy as jnp
        import numpy as np
        N_NODES = 6250
        N_EDGES = 100000
        D_IN = 128
        D_OUT = 128
        key = jax.random.key(seed)
        ks = jax.random.split(key, 6)
        x = jax.random.normal(ks[0], (N_NODES, D_IN), dtype=jnp.float32)
        edge_index = jax.random.randint(ks[1], (2, N_EDGES), 0, N_NODES, dtype=jnp.int32)
        s1 = 1.0 / np.sqrt(2 * D_IN)
        s2 = 1.0 / np.sqrt(D_IN)
        W1 = jax.random.normal(ks[2], (2 * D_IN, D_IN), dtype=jnp.float32) * s1
        b1 = jnp.zeros((D_IN,), dtype=jnp.float32)
        W2 = jax.random.normal(ks[3], (D_IN, 1), dtype=jnp.float32) * s2
        b2 = jnp.zeros((1,), dtype=jnp.float32)
        Wl = jax.random.normal(ks[4], (D_IN, D_OUT), dtype=jnp.float32) * s2
        bl = jnp.zeros((D_OUT,), dtype=jnp.float32)
        return {'x': x, 'edge_index': edge_index, 'W1': W1, 'b1': b1, 'W2': W2, 'b2': b2, 'Wl': Wl, 'bl': bl}
    _L0_gnn_all = _L0_gnn_setup()
    _L0_gnn_in = {k: v for k, v in _L0_gnn_all.items() if k in ('W1', 'b1', 'W2', 'b2', 'Wl', 'bl')}
    del _L0_gnn_all

    def _L1_gnn_setup():
        import jax, jax.numpy as jnp
        import numpy as np
        N = 6250
        E = 80000
        D = 128
        key = jax.random.key(seed)
        k1, k2, k3, k4 = jax.random.split(key, 4)
        x = jax.random.normal(k1, (N, D), dtype=jnp.float32)
        edge_index = jax.random.randint(k2, (2, E), 0, N, dtype=jnp.int64)
        W = jax.random.normal(k3, (D, D), dtype=jnp.float32) * (1.0 / np.sqrt(D))
        b = jax.random.normal(k4, (D,), dtype=jnp.float32) * 0.01
        return {'x': x, 'edge_index': edge_index, 'W': W, 'b': b}
    _L1_gnn_all = _L1_gnn_setup()
    _L1_gnn_in = {k: v for k, v in _L1_gnn_all.items() if k in ('W', 'b')}
    del _L1_gnn_all
    return {'x': x, 'src': src, 'dst': dst, 'L0_gnn_W1': _L0_gnn_in['W1'], 'L0_gnn_b1': _L0_gnn_in['b1'], 'L0_gnn_W2': _L0_gnn_in['W2'], 'L0_gnn_b2': _L0_gnn_in['b2'], 'L0_gnn_Wl': _L0_gnn_in['Wl'], 'L0_gnn_bl': _L0_gnn_in['bl'], 'L1_gnn_W': _L1_gnn_in['W'], 'L1_gnn_b': _L1_gnn_in['b']}

def reference(x, src, dst, L0_gnn_W1, L0_gnn_b1, L0_gnn_W2, L0_gnn_b2, L0_gnn_Wl, L0_gnn_bl, L1_gnn_W, L1_gnn_b):
    import jax
    import jax.numpy as jnp

    def _L0_gnn_ref(x, edge_index, W1, b1, W2, b2, Wl, bl):
        import jax, jax.numpy as jnp
        import numpy as np
        N_NODES = 6250
        N_EDGES = 100000
        D_IN = 128
        D_OUT = 128
        row, col = (edge_index[0], edge_index[1])
        n, d = x.shape
        xc = x[row]
        xn = x[col]
        h = jax.nn.relu(xc @ W1[:d] + xn @ W1[d:] + b1)
        mask = jax.nn.sigmoid(h @ W2 + b2)[:, 0]
        seg_sum = jax.ops.segment_sum(mask, row, num_segments=n)
        w = mask / (seg_sum[row] + 1e-09)
        agg = jax.ops.segment_sum(w[:, None] * xn, row, num_segments=n)
        deg = jax.ops.segment_sum(jnp.ones_like(mask), row, num_segments=n)
        out_emb = jnp.where((deg > 0)[:, None], 0.5 * x + 0.5 * agg, x)
        return jax.nn.relu(out_emb @ Wl + bl)

    def _L1_gnn_ref(x, edge_index, W, b):
        import jax, jax.numpy as jnp
        import numpy as np
        N = 6250
        E = 80000
        D = 128
        src = edge_index[0]
        dst = edge_index[1]
        n = x.shape[0]
        deg = jax.ops.segment_sum(jnp.ones((dst.shape[0],), dtype=x.dtype), dst, num_segments=n)
        deg_inv = jnp.where(deg > 0, 1.0 / deg, 0.0)
        edge_weight = deg_inv[dst]
        h = x @ W.T
        msg = h[src] * edge_weight[:, None]
        out = jax.ops.segment_sum(msg, dst, num_segments=n)
        return out + b
    edge_index = jnp.stack([src, dst])
    x = _layernorm(x + _L0_gnn_ref(x, edge_index, L0_gnn_W1, L0_gnn_b1, L0_gnn_W2, L0_gnn_b2, L0_gnn_Wl, L0_gnn_bl), axis=-1)
    x = _layernorm(x + _L1_gnn_ref(x, edge_index, L1_gnn_W, L1_gnn_b), axis=-1)
    return x

_drawn_inputs = setup_inputs


def setup_inputs(seed=0):
    import zlib

    import numpy as np

    out = dict(_drawn_inputs(seed))
    spreads = {'L0_gnn_b1': (0.0, 2.0), 'L0_gnn_bl': (0.0, 0.1)}
    factors = {'L0_gnn_W1': 2.708, 'L1_gnn_b': 5.73}
    for name, (base, spread) in spreads.items():
        noise = np.random.default_rng([zlib.crc32(name.encode()), seed]).standard_normal(out[name].shape)
        drawn = base * np.exp(spread * noise) if base else spread * noise
        out[name] = jnp.asarray(drawn.astype(out[name].dtype))
    for name, factor in factors.items():
        out[name] = (out[name] * factor).astype(out[name].dtype)
    return out
```

```python
from contextlib import ExitStack

import concourse.bass as bass
from concourse import mybir

F32 = mybir.dt.float32
BF16 = mybir.dt.bfloat16
I32 = mybir.dt.int32
ALU = mybir.AluOpType
ACT = mybir.ActivationFunctionType
AX_X = mybir.AxisListType.X

P = 128
N = 12500
D = 128
E = 200000
NB = -(-N // P)
NBX = NB + 1
ROWS = NBX * P
TAIL = N - (NB - 1) * P
PAD_KEY = NB * P

CW = E // P
REST = E - CW * P
ROUND = 4
K = 4
NQ = ROUND * -(-(CW + 1) // (K * ROUND))
NT = NQ * K
ROUNDS_SORT = NQ // ROUND
REAL_ROWS = CW + 1
NCH = -(-(REAL_ROWS + NB - 1) // P)
NPAIR = NCH * P
NG = NPAIR // K
HALVES = 2
SEG = D + 2
GW = 2 * D + 1
EPS = 1e-5
assert ROUNDS_SORT == NB and NG % ROUND == 0


def run_steps(eng, n, lag, step):
    head, rounds = 2, n // ROUND
    for s in range(head * ROUND):
        step(s // ROUND, s % ROUND)
    with eng.Fori(head, rounds) as r:
        for j in range(ROUND):
            step(r, j)
    for s in range(rounds * ROUND, n + lag):
        step(s // ROUND, s % ROUND)


def back(r, j, lag, n):
    r, j = r + (j - lag) // ROUND, (j - lag) % ROUND
    if isinstance(r, int) and not 0 <= r * ROUND + j < n:
        return None
    return r, j, r * ROUND + j


def span(start, size):
    return slice(start, start + size) if isinstance(start, int) else bass.ds(start, size)


def wait(eng, sem, value):
    if not isinstance(value, int) or value > 0:
        eng.wait_ge(sem, value)


def build(nc, x, src, dst, W1, b1, W2, b2, Wl, bl, W, b, out):
    with ExitStack() as ctx:
        def sb(name, shape, dt):
            return ctx.enter_context(nc.sbuf_tensor(name, shape, dt))

        def sem(name):
            return ctx.enter_context(nc.semaphore(name))

        def dram(name, shape, dt):
            return nc.dram_tensor(name, shape, dt).ap()

        table0 = dram("table0", (ROWS, 2 * D), F32)
        table1 = dram("table1", (ROWS, D), F32)
        lists = [dram(f"list{n}", (NT, 2 * P), I32) for n in range(2)]
        blocks_dram = [dram(f"blocks{n}", (NCH, P), I32) for n in range(2)]

        ident = sb("ident", [P, P], F32)
        ident_b = sb("ident_b", [P, P], BF16)
        ones = sb("ones", [P, P], F32)
        ones_b = sb("ones_b", [P, P], BF16)
        upper_b = sb("upper_b", [P, P], BF16)
        zeros = sb("zeros", [P, 2 * D], F32)
        iota_b = sb("iota_b", [P, P], BF16)
        iota_f = sb("iota_f", [P, P], F32)
        bound_f = sb("bound_f", [P, NBX], F32)
        bound_h = sb("bound_h", [P, NBX], F32)
        pair_no = sb("pair_no", [P, NCH], F32)
        w1 = sb("w1", [P, 2, D], F32)
        w2 = sb("w2", [P, D], F32)
        wl = sb("wl", [P, D], F32)
        w_in = sb("w_in", [P, D], F32)
        wt = sb("wt", [P, D], F32)
        b1_bc = sb("b1_bc", [P, D], F32)
        b2_bc = sb("b2_bc", [P, 1], F32)
        bl_bc = sb("bl_bc", [P, D], F32)
        b_bc = sb("b_bc", [P, D], F32)
        eps_c = sb("eps_c", [P, 1], F32)

        edge = [sb("edge_src", [P, NT], I32), sb("edge_dst", [P, NT], I32)]
        shift_tail = sb("shift_tail", [1, 2, REST], I32)
        hi = [sb("hi_src", [P, NT], BF16), sb("hi_dst", [P, NT], BF16)]
        below = [sb("below_src", [P, NBX], F32), sb("below_dst", [P, NBX], F32)]
        sign_sum = sb("sign_sum", [P, NBX], F32)
        start = [sb("start_src", [P, NBX + 1], F32), sb("start_dst", [P, NBX + 1], F32)]
        unsorted = sb("unsorted", [P, 2], F32)
        unsorted_i = sb("unsorted_i", [1, 1], I32)
        base = sb("base", [P, NBX], F32)
        hot = sb("hot", [P, 2, K, NBX], BF16)
        rank_prod = sb("rank_prod", [P, K, NBX], F32)
        pos = sb("pos", [P, ROUND, K], I32)
        rec = sb("rec", [P, ROUND, K, 2], I32)

        start_i = sb("start_i", [P, NBX + 1], I32)
        first_i = sb("first_i", [P, NBX + 1], I32)
        first_f = sb("first_f", [P, NBX + 1], F32)
        last_i = sb("last_i", [P, NBX], I32)
        last_f = sb("last_f", [P, NBX], F32)
        npair = sb("npair", [P, NB], F32)
        pair_end = sb("pair_end", [P, NB], F32)
        shift_f = sb("shift_f", [P, NBX], F32)
        pick = sb("pick", [P, NBX], F32)
        pair_block = sb("pair_block", [P, NCH], F32)
        pair_block_i = sb("pair_block_i", [P, NCH], I32)
        pair_lo = sb("pair_lo", [P, NCH], F32)
        pair_row = sb("pair_row", [P, NCH], F32)
        pair_row_i = sb("pair_row_i", [P, NCH], I32)
        blocks = sb("blocks", [1, NPAIR], I32)
        list_row = sb("list_row", [P, 2, P, 2], I32)
        list_f = sb("list_f", [P, 2, P], F32)
        local = sb("local", [P, NPAIR], F32)
        other = sb("other", [P, NPAIR], I32)

        a_tab = sb("a_tab", [P, NBX * D], F32)
        acc = sb("acc", [P, NBX * SEG], F32)
        acc_col = acc[:, :].rearrange("p (n s) -> p n s", s=SEG)
        keyf = [acc[:, n * NT:(n + 1) * NT] for n in range(2)]
        unused = [acc[:, n * NT:(n + 1) * NT] for n in (2, 3)]
        stage = acc[:, 4 * NT:6 * NT].bitcast(I32).rearrange("p (c f) -> p c f", f=2)
        shifted = acc[:, 6 * NT:6 * NT + CW].bitcast(I32)
        xb = sb("xb", [P, ROUND, D], F32)
        xbT = sb("xbT", [P, D], F32)
        bx = sb("bx", [P, D], F32)
        idx = sb("idx", [P, ROUND, K], I32)
        got = sb("got", [P, ROUND, K, GW], F32)
        hot_e = sb("hot_e", [P, ROUND, K, P], BF16)
        hot_n = sb("hot_n", [P, 2, K, P], F32)
        hidden = sb("hidden", [P, 2, K, D], F32)
        logit = sb("logit", [P, 2, K], F32)
        weight = sb("weight", [P, 2, K], F32)
        whot = sb("whot", [P, 2, K, P], F32)
        keep = sb("keep", [P, NBX], F32)
        scale = sb("scale", [P, NBX], F32)
        emb = sb("emb", [P, 2, D], F32)
        embT = sb("embT", [P, 2, D], F32)
        y = sb("y", [P, 2, D], F32)
        stats = sb("stats", [P, 2, 6], F32)
        mv = sb("mv", [P, 2, 2], F32)
        std = sb("std", [P, 2, 1], F32)
        rstd = sb("rstd", [P, 2, 1], F32)
        res = sb("res", [P, ROUND, D], F32)

        bank = [ctx.enter_context(nc.psum_tensor(f"bank{n}", [P, 512], F32)) for n in range(8)]
        bank_b = [t[:, 0:K * P // 2].bitcast(BF16) for t in bank]

        s_c = sem("constants")
        s_cv = sem("constants_vector")
        s_w = sem("weights_loaded")
        s_wt = sem("w_turned")
        s_wtc = sem("w_turned_copied")
        s_e = [sem("src_loaded"), sem("dst_loaded")]
        s_pad = sem("edge_padding")
        s_tab = sem("tables_filled")
        s_chain = sem("vector_chain")
        s_key = sem("keys_ready")
        s_thr = sem("sign_counts")
        s_bel = sem("below_counts")
        s_st = sem("starts_summed")
        s_start = sem("starts_ready")
        s_flag = sem("flag_ready")
        s_copy1 = sem("list1_written")
        s_list1 = sem("list1_ready")
        s_cnt1 = sem("dst_counted")
        s_cnt0 = sem("src_counted")
        s_flag0 = sem("descents_counted")
        s_ac = sem("half_bounds_ready")
        s_idb = sem("ident_bf16_ready")

        class SortSems:
            def __init__(self, tag):
                self.hot = sem(f"{tag}_hot_ready")
                self.rank = sem(f"{tag}_rank_ready")
                self.base = sem(f"{tag}_base_ready")
                self.prod = sem(f"{tag}_prod_ready")
                self.pos = sem(f"{tag}_pos_ready")
                self.rec = sem(f"{tag}_records_ready")
                self.go = sem(f"{tag}_scatter_go")
                self.wrote = [sem(f"{tag}_scattered{n}") for n in range(ROUND)]

        sort0, sort1 = SortSems("sort0"), SortSems("sort1")

        s_xld = sem("x_block_loaded")
        s_xT = sem("x_turned")
        s_xTc = sem("x_turned_copied")
        s_ab = sem("ab_ready")
        s_aw = sem("a_written")
        s_bw = sem("b_written")
        s_bst = sem("b_stored")

        class PairSems:
            def __init__(self, tag):
                self.calc = sem(f"{tag}_pairs_ready")
                self.bst = sem(f"{tag}_blocks_stored")
                self.bld = sem(f"{tag}_blocks_loaded")
                self.got = [sem(f"{tag}_rows_gathered{n}") for n in range(2)]
                self.flt = sem(f"{tag}_rows_float")
                self.turn = sem(f"{tag}_rows_turned")
                self.done = sem(f"{tag}_columns_ready")

        pair0, pair1 = PairSems("pair0"), PairSems("pair1")

        class EdgeSems:
            def __init__(self, tag):
                self.idx = sem(f"{tag}_idx_ready")
                self.go = sem(f"{tag}_gather_go")
                self.got = [sem(f"{tag}_gathered{n}") for n in range(ROUND)]
                self.hot = sem(f"{tag}_hot_ready")
                self.turn = sem(f"{tag}_hot_turned")
                self.turnc = sem(f"{tag}_hot_turned_copied")
                self.a = sem(f"{tag}_a_spread")
                self.hid = sem(f"{tag}_hidden_ready")
                self.logit = sem(f"{tag}_logit_ready")
                self.weight = sem(f"{tag}_weight_ready")
                self.whot = sem(f"{tag}_weighted_hot_ready")
                self.sum = sem(f"{tag}_pair_summed")
                self.acc = sem(f"{tag}_pair_added")

        edge0, edge1 = EdgeSems("edge0"), EdgeSems("edge1")

        class NodeSems:
            def __init__(self, tag):
                self.fac = sem(f"{tag}_factors_ready")
                self.x = [sem(f"{tag}_x_loaded{n}") for n in range(ROUND)]
                self.part = sem(f"{tag}_part_ready")
                self.emb = sem(f"{tag}_emb_ready")
                self.turn = sem(f"{tag}_emb_turned")
                self.turnc = sem(f"{tag}_emb_turned_copied")
                self.lin = sem(f"{tag}_linear_ready")
                self.lb = sem(f"{tag}_biased")
                self.y = sem(f"{tag}_y_ready")
                self.st = sem(f"{tag}_stats_ready")
                self.go = sem(f"{tag}_aggregate_go")
                self.mv = sem(f"{tag}_meanvar_ready")
                self.std = sem(f"{tag}_std_ready")
                self.rstd = sem(f"{tag}_rstd_ready")
                self.res = sem(f"{tag}_result_ready")
                self.out = [sem(f"{tag}_result_stored{n}") for n in range(ROUND)]

        node0, node1 = NodeSems("node0"), NodeSems("node1")

        def slot_use(r, lag=0):
            return (r + 1) * 16 * K

        def block_rows(table, nb, cols=None):
            view = table.rearrange("(n p) d -> n p d", p=P)
            return view[nb] if cols is None else view[nb, :, cols]

        SORT_LAG = 1
        EDGE_LAG = 4
        NODE_LAG = 3
        SPLIT = 45

        block = ctx.enter_context(nc.Block())

        @block.sync
        def _(sp):
            flat = [v.rearrange("(p c) -> p c", c=CW) for v in (src[0:P * CW], dst[0:P * CW])]
            sp.wait_ge(s_pad, 2)
            for n, v in enumerate((src, dst)):
                sp.dma_start(edge[n][:, 0:CW], flat[n]).then_inc(s_e[n], 16)
                sp.dma_start(edge[n][0:REST, CW:CW + 1],
                             v[P * CW:E].rearrange("(p c) -> p c", c=1)).then_inc(s_e[n], 16)
            sp.dma_start(shifted[:, :], dst[1:P * CW + 1].rearrange("(p c) -> p c", c=CW)).then_inc(s_e[1], 16)
            sp.dma_start(shift_tail[:, 0, 0:REST - 1], dst[P * CW:E - 1].rearrange("(a c) -> a c", a=1)).then_inc(s_e[1], 16)
            sp.dma_start(shift_tail[:, 1, 0:REST - 1], dst[P * CW + 1:E].rearrange("(a c) -> a c", a=1)).then_inc(s_e[1], 16)
            sp.dma_start(table0[0:N, D:2 * D], x).then_inc(s_tab, 16)
            sp.wait_ge(s_cv, 1)
            pad = ROWS - N
            sp.dma_start(table0[N:N + P, D:2 * D], zeros[:, 0:D]).then_inc(s_tab, 16)
            sp.dma_start(table0[N + P:ROWS, D:2 * D], zeros[0:pad - P, 0:D]).then_inc(s_tab, 16)
            sp.dma_start(block_rows(table0, NB, slice(0, D)), zeros[:, 0:D]).then_inc(s_tab, 16)
            sp.dma_start(block_rows(table1, NB), zeros[:, 0:D]).then_inc(s_tab, 16)
            sp.dma_start(w1[:, :, :], W1.rearrange("(t p) d -> p t d", p=P)).then_inc(s_w, 16)
            sp.dma_start(w2[:, :], W2.rearrange("d a -> a d").to_broadcast([P, D])).then_inc(s_w, 16)
            sp.dma_start(wl[:, :], Wl).then_inc(s_w, 16)
            sp.dma_start(w_in[:, :], W).then_inc(s_w, 16)
            for tile, v in ((b1_bc, b1), (bl_bc, bl), (b_bc, b), (b2_bc, b2)):
                sp.dma_start(tile[:, :], v.rearrange("(a d) -> a d", a=1).to_broadcast([P, v.shape[0]])).then_inc(s_w, 16)

            sp.wait_ge(s_copy1, 2)
            view = lists[1].rearrange("t (p c) -> (t p) c", c=2)
            sp.dma_start(view[0:P * CW, :].rearrange("(p c) f -> p (c f)", c=CW),
                         stage[:, 0:CW, :].rearrange("p c f -> p (c f)")).then_inc(s_list1, 16)
            sp.dma_start(view[P * CW:P * (CW + 1), :], stage[:, CW, :]).then_inc(s_list1, 16)

            sp.wait_ge(s_tab, 80)
            sp.dma_start(xb[:, 0, :], block_rows(table0, 0, slice(D, 2 * D))).then_inc(s_xld, 16)
            with sp.Fori(1, NB) as nb:
                sp.wait_ge(s_xT, nb)
                sp.dma_start(xb[:, 0, :], block_rows(table0, nb, slice(D, 2 * D))).then_inc(s_xld, 16)
                sp.wait_ge(s_bw, nb)
                sp.dma_start(block_rows(table0, nb - 1, slice(0, D)), bx[:, :]).then_inc(s_bst, 16)
            sp.wait_ge(s_bw, NB)
            sp.dma_start(block_rows(table0, NB - 1, slice(0, D)), bx[:, :]).then_inc(s_bst, 16)

            def pair_blocks(s, n):
                sp.wait_ge(s.calc, 1)
                with nc.allow_non_contiguous_dma(reason="13 columns of block numbers"):
                    sp.dma_start(blocks_dram[n].rearrange("c p -> p c"), pair_block_i[:, :]).then_inc(s.bst, 16)
                sp.wait_ge(s.bst, 16)
                sp.dma_start(blocks[:, :], blocks_dram[n].rearrange("(a c) p -> a (c p)", a=1)).then_inc(s.bld, 16)

            def node_io(s, table, cols, result, last_rows):
                def step(r, j):
                    at = back(r, j, 0, NB)
                    if at is not None:
                        r0, j0, nb = at
                        if not isinstance(r0, int) or r0 > 0:
                            sp.wait_ge(s.res, nb - ROUND + 1)
                        sp.dma_start(xb[:, j0, :], block_rows(table, nb, cols)).then_inc(s.x[j0], 16)
                    at = back(r, j, NODE_LAG, NB)
                    if at is not None:
                        r0, j0, nb = at
                        sp.wait_ge(s.res, nb + 1)
                        if isinstance(nb, int) and nb == NB - 1:
                            sp.dma_start(result[(NB - 1) * P:(NB - 1) * P + last_rows, :], res[0:last_rows, j0, :]).then_inc(s.out[j0], 16)
                        else:
                            view = result[0:(NB - 1) * P, :].rearrange("(n p) d -> n p d", p=P)
                            sp.dma_start(view[nb], res[:, j0, :]).then_inc(s.out[j0], 16)
                return step

            pair_blocks(pair0, 0)
            sp.wait_ge(edge0.acc, NPAIR)
            run_steps(sp, NB, NODE_LAG, node_io(node0, table0, slice(D, 2 * D), table1, P))
            sp.wait_ge(pair0.bld, 16)
            pair_blocks(pair1, 1)
            sp.wait_ge(edge1.acc, NPAIR)
            run_steps(sp, NB, NODE_LAG, node_io(node1, table1, slice(0, D), out, TAIL))
            for j in range(ROUND):
                sp.wait_ge(node1.out[j], 16 * len(range(j, NB, ROUND)))

        @block.gpsimd
        def _(pool):
            def ramp(tile, step, n, partition, base=0):
                pool.iota(tile[:, :], [[step, n]], base=base, channel_multiplier=partition,
                          allow_small_or_imprecise_dtypes=True).then_inc(s_c, 1)

            ramp(bound_f, P, NBX, 0)
            ramp(iota_f, 1, P, 0)
            ramp(iota_b, 1, P, 0)
            ramp(pair_no, P, NCH, 1)
            pool.wait_ge(s_cv, 3)
            pool.affine_select(out=ident[:, :], in_=zeros[:, 0:P], compare_op=ALU.not_equal, fill=1.0, base=0,
                               pattern=[[-1, P]], channel_multiplier=1).then_inc(s_c, 1)
            pool.affine_select(out=upper_b[:, :], in_=ones_b[:, :], compare_op=ALU.is_gt, fill=0.0, base=0,
                               pattern=[[1, P]], channel_multiplier=-1).then_inc(s_c, 1)

            def scatter(s, n):
                target = lists[n].rearrange("t (p c) -> (t p) c", c=2)
                def step(r, j):
                    q = r * ROUND + j
                    pool.wait_ge(s.pos, q + 1)
                    pool.wait_ge(s.rec, q + 1)
                    pool.sem_inc(s.go, 1)
                    for k in range(K):
                        pool.indirect_dma_start(target, bass.IndirectOffsetOnAxis(pos[:, j, k:k + 1], 0),
                                                rec[:, j, k, :], None).then_inc(s.wrote[j], 16)
                run_steps(pool, NQ, 0, step)
                for j in range(ROUND):
                    pool.wait_ge(s.wrote[j], slot_use(ROUNDS_SORT - 1))

            def gather_rows(s, n):
                pool.wait_ge(s.calc, 1)
                for c in range(NCH):
                    if c >= 2:
                        pool.wait_ge(s.flt, 2 * (c - 1))
                    pool.indirect_dma_start(list_row[:, c % 2, :, :].rearrange("p e f -> p (e f)"), None, lists[n],
                                            bass.IndirectOffsetOnAxis(pair_row_i[:, c:c + 1], 0)).then_inc(s.got[c % 2], 16)

            def gather_edges(s, table, width):
                def step(r, j):
                    pool.wait_ge(s.idx, r * ROUND + j + 1)
                    pool.sem_inc(s.go, 1)
                    for k in range(K):
                        off = 2 * D - width
                        pool.indirect_dma_start(got[:, j, k, off:off + width], None, table,
                                                bass.IndirectOffsetOnAxis(idx[:, j, k:k + 1], 0)).then_inc(s.got[j], 16)
                run_steps(pool, NG, 0, step)

            scatter(sort0, 0)
            gather_rows(pair0, 0)
            pool.wait_ge(s_bst, 16 * NB)
            gather_edges(edge0, table0, 2 * D)
            pool.wait_ge(s_flag, 1)
            pool.wait_ge(s_list1, 32)
            flag = pool.value_load(unsorted_i[0:1, 0:1], min_val=0, max_val=1)
            with pool.If(flag):
                scatter(sort1, 1)
            gather_rows(pair1, 1)
            for j in range(ROUND):
                pool.wait_ge(node0.out[j], 16 * len(range(j, NB, ROUND)))
            gather_edges(edge1, table1, D)

        @block.scalar
        def _(act):
            act.wait_ge(s_c, 1)
            act.activation(bound_h[:, :], bound_f[:, :], ACT.Copy, bias=-0.5).then_inc(s_ac, 1)
            act.wait_ge(s_ac, 1)
            act.wait_ge(s_key, 1)
            act.activation(unused[1], keyf[0], ACT.Sign, bias=bound_h[:, SPLIT:SPLIT + 1], scale=-1.0,
                           accum_out=sign_sum[:, SPLIT:SPLIT + 1]).then_inc(s_thr, 1)
            with act.Fori(SPLIT + 1, NBX) as nb:
                act.wait_ge(s_thr, nb - SPLIT)
                act.activation(unused[1], keyf[0], ACT.Sign, bias=bound_h[:, bass.ds(nb, 1)], scale=-1.0,
                               accum_out=sign_sum[:, bass.ds(nb, 1)]).then_inc(s_thr, 1)

            def sort_side(s, with_blocks):
                def step(r, j):
                    q = r * ROUND + j
                    if not (isinstance(r, int) and r < 1):
                        act.wait_ge(s.wrote[j], slot_use(r - 1))
                    for f in range(2):
                        act.copy(rec[:, j, :, f], edge[f][:, span(q * K, K)]).then_inc(s.rec, 1)
                    act.wait_ge(s.rank, q + 1)
                    act.wait_ge(s.base, q + 1)
                    act.copy(base[:, :], bank[j % 2][:, K * NBX:(K + 1) * NBX]).then_inc(s.base, 1)
                    if with_blocks and j == 0:
                        act.wait_ge(s_xT, r + 1)
                        wait(act, s_ab, r)
                        act.copy(xbT[:, :], bank[2][:, 0:P]).then_inc(s_xTc, 1)
                    if with_blocks and j == 2:
                        act.wait_ge(s_ab, r + 1)
                        wait(act, s_bst, 16 * r)
                        act.copy(bx[:, :], bank[4][:, 0:D]).then_inc(s_bw, 1)
                run_steps(act, NQ, 0, step)

            def pair_columns(s):
                for c in range(NCH):
                    act.wait_ge(s.turn, c + 1)
                    act.copy(local[:, c * P:(c + 1) * P], bank[4][:, 0:P]).then_inc(s.done, 1)
                    act.copy(other[:, c * P:(c + 1) * P], bank[4][:, P:2 * P]).then_inc(s.done, 1)

            def indices(s, r, j):
                at = back(r, j, 0, NG)
                if at is not None:
                    g = at[2]
                    wait(act, s.sum, HALVES * (g - ROUND + 1))
                    act.copy(idx[:, j, :], other[:, span(g * K, K)]).then_inc(s.idx, 1)

            def edge0_step(r, j):
                indices(edge0, r, j)
                at = back(r, j, 2, NG)
                if at is not None:
                    _, jj, g = at
                    act.wait_ge(edge0.logit, g + 1)
                    act.activation(weight[:, jj % 2, :], logit[:, jj % 2, :], ACT.Sigmoid, bias=b2_bc[:, :]).then_inc(edge0.weight, 1)
                    act.wait_ge(edge0.weight, g + 1)
                    wait(act, edge0.sum, HALVES * (g - 1))
                    for k in range(K):
                        last = act.activation(whot[:, jj % 2, k, :], hot_e[:, jj, k, :], ACT.Copy,
                                              scale=weight[:, jj % 2, k:k + 1])
                    last.then_inc(edge0.whot, 1)
                at = back(r, j, 0, NG)
                if at is not None:
                    g = at[2]
                    act.wait_ge(edge0.turn, g + 1)
                    wait(act, edge0.a, g - 1)
                    act.copy(hot_n[:, j % 2, :, :].rearrange("p k n -> p (k n)"), bank_b[j % 2]).then_inc(edge0.turnc, 1)

            def node_side(s):
                def step(r, j):
                    at = back(r, j, 0, NB)
                    if at is not None:
                        _, jj, nb = at
                        act.wait_ge(s.turn, nb + 1)
                        wait(act, s.lin, nb - 1)
                        act.copy(embT[:, jj % 2, :], bank[jj % 2][:, 0:P]).then_inc(s.turnc, 1)
                    at = back(r, j, 1, NB)
                    if at is not None:
                        _, jj, nb = at
                        act.wait_ge(s.mv, nb + 1)
                        wait(act, s.rstd, nb - 1)
                        act.activation(std[:, jj % 2, :], mv[:, jj % 2, 1:2], ACT.Sqrt, bias=eps_c[:, :]).then_inc(s.std, 1)
                run_steps(act, NB, 1, step)

            for n in range(2):
                act.wait_ge(s_e[n], (32, 80)[n])
            sort_side(sort0, True)
            pair_columns(pair0)
            act.wait_ge(s_w, 16 * 8)
            run_steps(act, NG, 2, edge0_step)
            act.wait_ge(s_flag, 1)
            flag = act.value_load(unsorted_i[0:1, 0:1], min_val=0, max_val=1)
            with act.If(flag):
                for j in range(ROUND):
                    act.wait_ge(sort0.wrote[j], slot_use(ROUNDS_SORT - 1))
                sort_side(sort1, False)
            act.wait_ge(edge0.sum, HALVES * NG)
            pair_columns(pair1)
            node_side(node0)
            run_steps(act, NG, 0, lambda r, j: indices(edge1, r, j))
            node_side(node1)

        @block.tensor
        def _(pe):
            regs = [pe.alloc_register(f"pe_block{k}") for k in range(K)]

            pe.wait_ge(s_cv, 3)
            pe.wait_ge(s_c, 6)
            pe.wait_ge(s_idb, 1)
            pe.wait_ge(s_bel, 1)
            pe.matmul(bank[0][:, 0:NBX], ones[:, :], below[0][:, :], start=True, stop=True).then_inc(s_st, 1)
            pe.wait_ge(s_flag0, 1)
            pe.matmul(bank[1][:, 0:2], ones[:, :], unsorted[:, :], start=True, stop=True).then_inc(s_st, 1)
            pe.wait_ge(s_w, 16 * 8)
            pe.transpose(bank[2][:, 0:P], w_in[:, :], ident[:, :]).then_inc(s_wt, 1)
            pe.wait_ge(s_wtc, 1)

            def ranks(s, with_blocks):
                def step(r, j):
                    q = r * ROUND + j
                    view = bank[j % 2][:, 0:(K + 1) * NBX].rearrange("p (k n) -> p k n", n=NBX)
                    pe.wait_ge(s.hot, q + 1)
                    pe.wait_ge(s.base, q + 1)
                    wait(pe, s.prod, q - 1)
                    pe.matmul(view, ident[:, :], base[:, :].rearrange("p (a n) -> p a n", a=1).to_broadcast([P, K + 1, NBX]),
                              start=True, stop=False)
                    pe.matmul(view[:, 0:K, :], upper_b[:, :], hot[:, j % 2, :, :], start=False, stop=False)
                    for k in range(K):
                        last = pe.matmul(view[:, k + 1:K + 1, :], ones_b[:, :],
                                         hot[:, j % 2, k:k + 1, :].to_broadcast([P, K - k, NBX]),
                                         start=False, stop=(k == K - 1))
                    last.then_inc(s.rank, 1)
                    if with_blocks and j == 0:
                        pe.wait_ge(s_xld, 16 * (r + 1))
                        wait(pe, s_xTc, r)
                        pe.transpose(bank[2][:, 0:P], xb[:, 0, :], ident[:, :]).then_inc(s_xT, 1)
                    if with_blocks and j == 1:
                        pe.wait_ge(s_xTc, r + 1)
                        wait(pe, s_aw, r)
                        pe.matmul(bank[3][:, 0:D], xbT[:, :], w1[:, 0, :], start=True, stop=True)
                        wait(pe, s_bw, r)
                        pe.matmul(bank[4][:, 0:D], xbT[:, :], w1[:, 1, :], start=True, stop=True).then_inc(s_ab, 1)
                run_steps(pe, NQ, 0, step)

            def turn_rows(s):
                for c in range(NCH):
                    pe.wait_ge(s.flt, 2 * (c + 1))
                    if c:
                        pe.wait_ge(s.done, 2 * c)
                    pe.transpose(bank[4][:, 0:P], list_f[:, 0, :], ident[:, :])
                    pe.transpose(bank[4][:, P:2 * P], list_f[:, 1, :], ident[:, :]).then_inc(s.turn, 1)

            def sums(s, r, j, lag, lhs, count):
                at = back(r, j, lag, NG)
                if at is None:
                    return
                rr, jj, g = at
                pe.wait_ge(s.got[jj], slot_use(rr))
                for k in range(K):
                    h, i = k // (K // HALVES), k % (K // HALVES)
                    if i == 0:
                        wait(pe, s.acc, K * (g - 2) + (h + 1) * (K // HALVES))
                    area = bank[4 + HALVES * (jj % 2) + h][:, i * SEG:(i + 1) * SEG]
                    last = pe.matmul(area[:, 0:D + 1], lhs(jj, k), got[:, jj, k, D:2 * D + 1], start=True, stop=True)
                    if count:
                        last = pe.matmul(area[:, D + 1:D + 2], hot_e[:, jj, k, :], ones_b[:, 0:1], start=True, stop=True)
                    if i == K // HALVES - 1:
                        last.then_inc(s.sum, 1)

            def edge0_step(r, j):
                at = back(r, j, 1, NG)
                if at is not None:
                    _, jj, g = at
                    pe.load(regs, blocks[0:1, span(g * K, K)])
                    nbs = [pe.snap(v, min_val=0, max_val=NB) for v in regs]
                    pe.wait_ge(edge0.turnc, g + 1)
                    wait(pe, edge0.hid, g - 1)
                    for k in range(K):
                        last = pe.matmul(bank[2 + jj % 2][:, k * D:(k + 1) * D], hot_n[:, jj % 2, k, :],
                                         a_tab[:, bass.ds(nbs[k] * D, D)], start=True, stop=True)
                    last.then_inc(edge0.a, 1)
                at = back(r, j, 3, NG)
                if at is not None:
                    pe.wait_ge(edge0.whot, at[2] + 1)
                sums(edge0, r, j, 3, lambda jj, k: whot[:, jj % 2, k, :], True)
                at = back(r, j, 0, NG)
                if at is not None:
                    g = at[2]
                    pe.wait_ge(edge0.hot, g + 1)
                    wait(pe, edge0.turnc, g - 1)
                    for k in range(K):
                        last = pe.transpose(bank_b[j % 2][:, k * P:(k + 1) * P], hot_e[:, j, k, :], ident_b[:, :])
                    last.then_inc(edge0.turn, 1)

            def edge1_step(r, j):
                at = back(r, j, 1, NG)
                if at is not None:
                    pe.wait_ge(edge1.hot, at[2] + 1)
                sums(edge1, r, j, 1, lambda jj, k: whot[:, jj % 2, k, :], False)

            def linear(s, weights):
                def step(r, j):
                    at = back(r, j, 0, NB)
                    if at is not None:
                        _, jj, nb = at
                        pe.wait_ge(s.emb, nb + 1)
                        wait(pe, s.turnc, nb - 1)
                        pe.transpose(bank[jj % 2][:, 0:P], emb[:, jj % 2, :], ident[:, :]).then_inc(s.turn, 1)
                    at = back(r, j, 1, NB)
                    if at is not None:
                        _, jj, nb = at
                        pe.wait_ge(s.turnc, nb + 1)
                        wait(pe, s.lb, nb - 1)
                        pe.matmul(bank[2 + jj % 2][:, 0:D], embT[:, jj % 2, :], weights[:, :],
                                  start=True, stop=True).then_inc(s.lin, 1)
                run_steps(pe, NB, 1, step)

            pe.wait_ge(sort0.base, 1)
            pe.wait_ge(s_flag, 1)
            ranks(sort0, True)
            pe.wait_ge(s_bel, 2)
            pe.wait_ge(s_aw, NB)
            pe.matmul(bank[3][:, 0:NBX], ones[:, :], below[1][:, :], start=True, stop=True).then_inc(s_st, 1)
            pe.wait_ge(s_bw, NB)
            turn_rows(pair0)
            pe.wait_ge(pair0.bld, 16)
            run_steps(pe, NG, 3, edge0_step)
            flag = pe.value_load(unsorted_i[0:1, 0:1], min_val=0, max_val=1)
            with pe.If(flag):
                ranks(sort1, False)
            turn_rows(pair1)
            linear(node0, wl)
            run_steps(pe, NG, 1, edge1_step)
            linear(node1, wt)

        @block.vector
        def _(v):
            regs = [v.alloc_register(f"v_block{k}") for k in range(K)]
            links = 0

            def link(ins):
                nonlocal links
                links += 1
                ins.then_inc(s_chain, 1)
                v.wait_ge(s_chain, links)

            for n in range(2):
                v.memset(edge[n][:, CW:NT], PAD_KEY).then_inc(s_pad, 1)
            v.memset(zeros[:, :], 0.0).then_inc(s_cv, 1)
            v.memset(ones[:, :], 1.0).then_inc(s_cv, 1)
            v.memset(ones_b[:, :], 1.0).then_inc(s_cv, 1)
            v.memset(eps_c[:, :], EPS)
            v.memset(got[:, :, :, 2 * D:2 * D + 1], 1.0)
            v.memset(a_tab[:, NB * D:NBX * D], 0.0)
            link(v.memset(unsorted[:, :], 0.0))

            for n in range(2):
                v.wait_ge(s_e[n], (32, 80)[n])
                v.tensor_copy(keyf[n], edge[n][:, :]).then_inc(s_key, 1)
                link(v.tensor_scalar(other[:, 0:NT], edge[n][:, :], 7, None, ALU.arith_shift_right))
                link(v.tensor_copy(hi[n][:, :], other[:, 0:NT]))
            v.wait_ge(s_c, 6)
            v.tensor_copy(ident_b[:, :], ident[:, :]).then_inc(s_idb, 1)

            def count(n, nb):
                return v.tensor_scalar(unused[0], keyf[n], bound_f[:, span(nb, 1)], None, ALU.is_lt, ALU.add,
                                       accum_out=below[n][:, span(nb, 1)])

            count(0, 0).then_inc(s_cnt0, 1)
            with v.Fori(1, SPLIT) as nb:
                v.wait_ge(s_cnt0, nb)
                count(0, nb).then_inc(s_cnt0, 1)
            v.wait_ge(s_cnt0, SPLIT)
            v.wait_ge(s_thr, NBX - SPLIT)
            v.tensor_scalar(below[0][:, SPLIT:NBX], sign_sum[:, SPLIT:NBX], 0.5, NT / 2, ALU.mult, ALU.add).then_inc(s_bel, 1)
            link(v.scalar_tensor_tensor(out=unused[0][:, 0:CW], in0=shifted, scalar=0.0, in1=edge[1][:, 0:CW],
                                        op0=ALU.add, op1=ALU.is_lt, accum_out=unsorted[:, 0:1]))
            v.scalar_tensor_tensor(out=unused[0][0:1, 0:REST - 1], in0=shift_tail[:, 1, 0:REST - 1], scalar=0.0,
                                   in1=shift_tail[:, 0, 0:REST - 1], op0=ALU.add, op1=ALU.is_lt,
                                   accum_out=unsorted[0:1, 1:2]).then_inc(s_flag0, 1)
            v.wait_ge(s_st, 1)
            v.tensor_copy(start[0][:, 0:NBX], bank[0][:, 0:NBX])
            v.tensor_copy(base[:, :], bank[0][:, 0:NBX]).then_inc(sort0.base, 1)
            v.wait_ge(s_st, 2)
            link(v.tensor_reduce(unsorted[:, 0:1], bank[1][:, 0:2], AX_X, ALU.add))
            v.tensor_scalar(unsorted_i[:, :], unsorted[0:1, 0:1], 1.0, None, ALU.min).then_inc(s_flag, 1)
            for f in range(2):
                v.tensor_copy(stage[:, :, f], edge[f][:, :]).then_inc(s_copy1, 1)
            v.wait_ge(s_wt, 1)
            v.tensor_copy(wt[:, :], bank[2][:, 0:P]).then_inc(s_wtc, 1)
            v.wait_ge(s_w, 16 * 8)

            def places(s, n, with_blocks):
                def step(r, j):
                    at = back(r, j, 0, NQ)
                    if at is not None:
                        q = at[2]
                        wait(v, s.rank, q - 1)
                        wait(v, s.prod, q - 1)
                        v.tensor_tensor(hot[:, j % 2, :, :],
                                        hi[n][:, span(q * K, K)].rearrange("p (k a) -> p k a", a=1).to_broadcast([P, K, NBX]),
                                        iota_b[:, 0:NBX].rearrange("p (a n) -> p a n", a=1).to_broadcast([P, K, NBX]),
                                        ALU.is_equal).then_inc(s.hot, 1)
                    at = back(r, j, 1, NQ)
                    if at is not None:
                        rr, jj, q = at
                        v.wait_ge(s.base, q + 2)
                        wait(v, s.pos, q)
                        v.tensor_tensor(rank_prod[:, :, :], hot[:, jj % 2, :, :],
                                        bank[jj % 2][:, 0:K * NBX].rearrange("p (k n) -> p k n", n=NBX),
                                        ALU.mult).then_inc(s.prod, 1)
                        if with_blocks and j == 2:
                            v.wait_ge(s_ab, r + 1)
                            v.tensor_tensor(a_tab[:, span(r * D, D)], bank[3][:, 0:D], b1_bc[:, :], ALU.add).then_inc(s_aw, 1)
                        if with_blocks and j == 3:
                            wait(v, s_cnt1, r)
                            count(1, r).then_inc(s_cnt1, 1)
                        v.wait_ge(s.prod, q + 1)
                        if not (isinstance(rr, int) and rr < 1):
                            v.wait_ge(s.wrote[jj], slot_use(rr - 1))
                        with nc.allow_low_precision(reason="places are whole numbers below 2 ** 24"):
                            v.tensor_reduce(pos[:, jj, :], rank_prod[:, :, :], AX_X, ALU.add).then_inc(s.pos, 1)
                run_steps(v, NQ, SORT_LAG, step)

            def pairs(s, n):
                st = start[n]
                link(v.tensor_copy(start_i[:, 0:NBX], st[:, 0:NBX]))
                link(v.tensor_scalar(first_i[:, 0:NBX], start_i[:, 0:NBX], 7, None, ALU.arith_shift_right))
                link(v.tensor_copy(first_f[:, 0:NBX], first_i[:, 0:NBX]))
                link(v.tensor_scalar(start_i[:, 0:NB], st[:, 1:NBX], -1.0, None, ALU.add))
                link(v.tensor_scalar(last_i[:, 0:NB], start_i[:, 0:NB], 7, None, ALU.arith_shift_right))
                link(v.tensor_copy(last_f[:, 0:NB], last_i[:, 0:NB]))
                link(v.tensor_tensor(last_f[:, 0:NB], last_f[:, 0:NB], first_f[:, 0:NB], ALU.subtract))
                link(v.tensor_tensor(pick[:, 0:NB], st[:, 1:NBX], st[:, 0:NB], ALU.is_gt))
                link(v.scalar_tensor_tensor(out=npair[:, :], in0=last_f[:, 0:NB], scalar=1.0, in1=pick[:, 0:NB],
                                            op0=ALU.add, op1=ALU.mult))
                link(v.tensor_tensor_scan(pair_end[:, :], npair[:, :], zeros[:, 0:NB], 0.0, ALU.add, ALU.add))
                link(v.memset(shift_f[:, :], -4.0 * NPAIR))
                link(v.tensor_tensor(shift_f[:, 0:NB], first_f[:, 0:NB], pair_end[:, :], ALU.subtract))
                link(v.tensor_tensor(shift_f[:, 0:NB], shift_f[:, 0:NB], npair[:, :], ALU.add))
                for c in range(NCH):
                    link(v.tensor_scalar(pick[:, 0:NB], pair_end[:, :], pair_no[:, c:c + 1], None, ALU.is_le, ALU.add,
                                         accum_out=pair_block[:, c:c + 1]))
                    link(v.scalar_tensor_tensor(out=pick[:, :], in0=iota_f[:, 0:NBX], scalar=pair_block[:, c:c + 1],
                                                in1=shift_f[:, :], op0=ALU.is_equal, op1=ALU.mult,
                                                accum_out=pair_row[:, c:c + 1]))
                link(v.tensor_tensor(pair_row[:, :], pair_row[:, :], pair_no[:, :], ALU.add))
                link(v.tensor_scalar(pair_row[:, :], pair_row[:, :], 0.0, REAL_ROWS - 1.0, ALU.max, ALU.min))
                v.tensor_copy(pair_row_i[:, :], pair_row[:, :])
                v.tensor_scalar(pair_lo[:, :], pair_block[:, :], float(P), None, ALU.mult)
                v.tensor_copy(pair_block_i[:, :], pair_block[:, :]).then_inc(s.calc, 1)
                v.wait_ge(s.calc, 1)

            def rows_float(s, field):
                for c in range(NCH):
                    v.wait_ge(s.got[c % 2], 16 * (c // 2 + 1))
                    if c:
                        v.wait_ge(s.turn, c)
                    v.tensor_scalar(list_f[:, 0, :], list_row[:, c % 2, :, field], pair_lo[:, c:c + 1], None,
                                    ALU.subtract).then_inc(s.flt, 1)
                    v.tensor_copy(list_f[:, 1, :], list_row[:, c % 2, :, 1 - field]).then_inc(s.flt, 1)

            def one_hots(s, r, j, out, free):
                at = back(r, j, 0, NG)
                if at is not None:
                    g = at[2]
                    wait(v, s.sum, HALVES * (g - free + 1))
                    for k in range(K):
                        last = v.tensor_scalar(out(k), iota_b[:, :], local[:, span(g * K + k, 1)], None, ALU.is_equal)
                    last.then_inc(s.hot, 1)

            def add_sums(s, r, j, lag, cols, between=None):
                at = back(r, j, lag, NG)
                if at is not None:
                    g = at[2]
                    v.load(regs, blocks[0:1, span(g * K, K)])
                    nbs = [v.snap(x_, min_val=0, max_val=NB) for x_ in regs]
                for k in range(K):
                    h, i = k // (K // HALVES), k % (K // HALVES)
                    if between is not None:
                        between(k)
                    if at is not None:
                        v.wait_ge(s.sum, HALVES * g + h + 1)
                        wait(v, s.acc, K * g + k)
                        here = acc[:, bass.ds(nbs[k] * SEG, cols)]
                        v.tensor_tensor(here, here, bank[4 + HALVES * (at[1] % 2) + h][:, i * SEG:i * SEG + cols],
                                        ALU.add).then_inc(s.acc, 1)

            def edge0_step(r, j):
                one_hots(edge0, r, j, lambda k: hot_e[:, j, k, :], ROUND)
                at = back(r, j, 2, NG)
                if at is not None:
                    rr, jj, g = at
                    v.wait_ge(edge0.a, g + 1)
                    v.wait_ge(edge0.got[jj], slot_use(rr))
                    wait(v, edge0.logit, g - 1)
                    v.tensor_tensor(hidden[:, jj % 2, :, :],
                                    bank[2 + jj % 2][:, :].rearrange("p (k d) -> p k d", d=D),
                                    got[:, jj, :, 0:D], ALU.add).then_inc(edge0.hid, 1)
                    wait(v, edge0.weight, g - 1)

                def logits(k):
                    if at is not None:
                        if k == 0:
                            v.wait_ge(edge0.hid, at[2] + 1)
                        h = hidden[:, at[1] % 2, k, :]
                        ins = v.scalar_tensor_tensor(out=h, in0=h, scalar=0.0, in1=w2[:, :], op0=ALU.max, op1=ALU.mult,
                                                     accum_out=logit[:, at[1] % 2, k:k + 1])
                        if k == K - 1:
                            ins.then_inc(edge0.logit, 1)

                add_sums(edge0, r, j, 4, SEG, logits)

            def edge1_step(r, j):
                one_hots(edge1, r, j, lambda k: whot[:, j % 2, k, :], 2)
                add_sums(edge1, r, j, 2, D + 1)

            def nodes(s, layer):
                bias = (bl_bc, b_bc)[layer]
                def step(r, j):
                    at = back(r, j, 0, NB)
                    if at is not None:
                        _, jj, nb = at
                        wait(v, s.turn, nb - 1)
                        mean = acc[:, span(nb * SEG, D)]
                        if layer == 0:
                            v.wait_ge(s.x[jj], 16 * (at[0] + 1))
                            v.tensor_scalar(emb[:, jj % 2, :], xb[:, jj, :], keep[:, span(nb, 1)], None,
                                            ALU.mult).then_inc(s.part, 1)
                            v.wait_ge(s.part, nb + 1)
                            v.scalar_tensor_tensor(out=emb[:, jj % 2, :], in0=mean, scalar=scale[:, span(nb, 1)],
                                                   in1=emb[:, jj % 2, :], op0=ALU.mult, op1=ALU.add).then_inc(s.emb, 1)
                        else:
                            v.tensor_scalar(emb[:, jj % 2, :], mean, scale[:, span(nb, 1)], None,
                                            ALU.mult).then_inc(s.emb, 1)
                    at = back(r, j, 1, NB)
                    if at is not None:
                        rr, jj, nb = at
                        h = jj % 2
                        wait(v, s.res, nb - 1)
                        v.wait_ge(s.lin, nb + 1)
                        v.wait_ge(s.x[jj], 16 * (rr + 1))
                        v.tensor_tensor(y[:, h, :], bank[2 + h][:, 0:D], bias[:, :], ALU.add).then_inc(s.lb, 1)
                        v.wait_ge(s.lb, nb + 1)
                        if layer == 0:
                            v.scalar_tensor_tensor(out=y[:, h, :], in0=y[:, h, :], scalar=0.0, in1=xb[:, jj, :],
                                                   op0=ALU.max, op1=ALU.add).then_inc(s.y, 1)
                        else:
                            v.tensor_tensor(y[:, h, :], y[:, h, :], xb[:, jj, :], ALU.add).then_inc(s.y, 1)
                        v.wait_ge(s.y, nb + 1)
                        v.bn_stats(stats[:, h, :], y[:, h, :]).then_inc(s.st, 1)
                        v.wait_ge(s.st, nb + 1)
                        wait(v, s.std, nb - 1)
                        v.sem_inc(s.go, 1)
                        v.bn_aggr(mv[:, h, :], stats[:, h, :]).then_inc(s.mv, 1)
                    at = back(r, j, 2, NB)
                    if at is not None:
                        rr, jj, nb = at
                        h = jj % 2
                        v.wait_ge(s.std, nb + 1)
                        v.reciprocal(rstd[:, h, :], std[:, h, :]).then_inc(s.rstd, 1)
                        v.wait_ge(s.rstd, nb + 1)
                        if not (isinstance(rr, int) and rr < 1):
                            v.wait_ge(s.out[jj], 16 * rr)
                        v.tensor_scalar(res[:, jj, :], y[:, h, :], mv[:, h, 0:1], rstd[:, h, :], ALU.subtract,
                                        ALU.mult).then_inc(s.res, 1)
                run_steps(v, NB, 2, step)

            places(sort0, 0, True)
            v.wait_ge(s_cnt1, NB)
            count(1, NB).then_inc(s_bel, 1)
            pairs(pair0, 0)
            rows_float(pair0, 0)
            v.wait_ge(s_st, 3)
            link(v.tensor_copy(start[1][:, 0:NBX], bank[3][:, 0:NBX]))
            v.wait_ge(s_bel, 2)
            v.wait_ge(s_list1, 32)
            link(v.memset(acc[:, :], 0.0))
            v.wait_ge(pair0.bld, 16)
            v.wait_ge(pair0.done, 2 * NCH)
            run_steps(v, NG, 4, edge0_step)

            flag = v.value_load(unsorted_i[0:1, 0:1], min_val=0, max_val=1)
            with v.If(flag):
                for j in range(ROUND):
                    v.wait_ge(sort0.wrote[j], slot_use(ROUNDS_SORT - 1))
                v.wait_ge(sort0.base, NQ + 1)
                v.tensor_copy(base[:, :], start[1][:, 0:NBX]).then_inc(sort1.base, 1)
                places(sort1, 1, False)
            v.wait_ge(edge0.acc, NPAIR)
            pairs(pair1, 1)
            rows_float(pair1, 1)

            link(v.tensor_scalar(scale[:, :], acc_col[:, :, D], 1e-9, None, ALU.add))
            link(v.reciprocal(scale[:, :], scale[:, :]))
            link(v.tensor_scalar(keep[:, :], acc_col[:, :, D + 1], 0.0, 0.5, ALU.is_gt, ALU.mult))
            link(v.tensor_tensor(scale[:, :], scale[:, :], keep[:, :], ALU.mult))
            link(v.tensor_scalar(keep[:, :], keep[:, :], -1.0, 1.0, ALU.mult, ALU.add))
            nodes(node0, 0)
            v.wait_ge(node0.emb, NB)
            link(v.memset(acc[:, :], 0.0))
            v.wait_ge(pair1.done, 2 * NCH)
            v.wait_ge(pair1.bld, 16)
            run_steps(v, NG, 2, edge1_step)
            v.wait_ge(edge1.acc, NPAIR)
            link(v.tensor_scalar(scale[:, :], acc_col[:, :, D], 1.0, None, ALU.max))
            link(v.reciprocal(scale[:, :], scale[:, :]))
            link(v.tensor_scalar(keep[:, :], acc_col[:, :, D], 0.0, None, ALU.is_gt))
            link(v.tensor_tensor(scale[:, :], scale[:, :], keep[:, :], ALU.mult))
            nodes(node1, 1)


_INS = ["x", "src", "dst", "L0_gnn_W1", "L0_gnn_b1", "L0_gnn_W2", "L0_gnn_b2", "L0_gnn_Wl", "L0_gnn_bl", "L1_gnn_W", "L1_gnn_b"]


def kernel(**inputs):
    import numpy as _np
    import concourse.bacc as _bacc
    from concourse import mybir as _mybir
    from concourse.bass_utils import run_bass_kernel_spmd as _run

    nc = _bacc.Bacc("TRN2", target_bir_lowering=False, num_devices=1)
    arrays, args = {}, []
    for name in _INS:
        a = _np.ascontiguousarray(inputs[name])
        arrays[f"in_{name}_dram"] = a
        args.append(nc.dram_tensor(f"in_{name}_dram", a.shape, _mybir.dt.from_np(a.dtype), kind="ExternalInput").ap())
    out = nc.dram_tensor("out_0_dram", (N, D), _mybir.dt.float32, kind="ExternalOutput").ap()
    build(nc, *args, out)
    r = _run(nc, [arrays], core_ids=[0])
    return r.results[0]["out_0_dram"]
```

```python
from contextlib import ExitStack

import concourse.bass as bass
from concourse import mybir

F32 = mybir.dt.float32
BF16 = mybir.dt.bfloat16
I32 = mybir.dt.int32
ALU = mybir.AluOpType
ACT = mybir.ActivationFunctionType
AX_X = mybir.AxisListType.X

P = 128
N = 12500
D = 128
E = 200000
NB = -(-N // P)
NBX = NB + 1
ROWS = NBX * P
TAIL = N - (NB - 1) * P
PAD_KEY = NB * P

CW = E // P
REST = E - CW * P
ROUND = 4
K = 4
NQ = ROUND * -(-(CW + 1) // (K * ROUND))
NT = NQ * K
ROUNDS_SORT = NQ // ROUND
REAL_ROWS = CW + 1
NCH = -(-(REAL_ROWS + NB - 1) // P)
NPAIR = NCH * P
NG = NPAIR // K
NTICK = NG // ROUND + 2
HALVES = 2
SEG = D + 2
LIN_AT = K // 2 * SEG
GW = 2 * D + 1
EPS = 1e-5
assert ROUNDS_SORT == NB and NG % ROUND == 0 and NTICK <= P


def run_steps(eng, n, lag, step, per=ROUND):
    head, rounds = 2, n // per
    for s in range(head * per):
        step(s // per, s % per)
    with eng.Fori(head, rounds) as r:
        for j in range(per):
            step(r, j)
    for s in range(rounds * per, n + lag):
        step(s // per, s % per)


def back(r, j, lag, n, per=ROUND):
    r, j = r + (j - lag) // per, (j - lag) % per
    if isinstance(r, int) and not 0 <= r * per + j < n:
        return None
    return r, j, r * per + j


def span(start, size):
    return slice(start, start + size) if isinstance(start, int) else bass.ds(start, size)


def wait(eng, sem, value):
    if not isinstance(value, int) or value > 0:
        eng.wait_ge(sem, value)


def build(nc, x, src, dst, W1, b1, W2, b2, Wl, bl, W, b, out):
    with ExitStack() as ctx:
        def sb(name, shape, dt):
            return ctx.enter_context(nc.sbuf_tensor(name, shape, dt))

        def sem(name):
            return ctx.enter_context(nc.semaphore(name))

        def dram(name, shape, dt):
            return nc.dram_tensor(name, shape, dt).ap()

        table0 = dram("table0", (ROWS, 2 * D), F32)
        table1 = dram("table1", (ROWS, D), F32)
        lists = [dram(f"list{n}", (NT, 2 * P), I32) for n in range(2)]
        blocks_dram = [dram(f"blocks{n}", (NCH, P), I32) for n in range(2)]

        ident = sb("ident", [P, P], F32)
        ident_b = sb("ident_b", [P, P], BF16)
        ones = sb("ones", [P, P], F32)
        ones_b = sb("ones_b", [P, P], BF16)
        upper_b = sb("upper_b", [P, P], BF16)
        zeros = sb("zeros", [P, 2 * D], F32)
        iota_b = sb("iota_b", [P, P], BF16)
        iota_f = sb("iota_f", [P, P], F32)
        bound_f = sb("bound_f", [P, NBX], F32)
        bound_h = sb("bound_h", [P, NBX], F32)
        pair_no = sb("pair_no", [P, NCH], F32)
        turn_no = sb("turn_no", [P, 2], F32)
        w1 = sb("w1", [P, 2, D], F32)
        w2 = sb("w2", [P, D], F32)
        wl = sb("wl", [P, D], F32)
        w_in = sb("w_in", [P, D], F32)
        wt = sb("wt", [P, D], F32)
        b1_bc = sb("b1_bc", [P, D], F32)
        b2_bc = sb("b2_bc", [P, 1], F32)
        bl_bc = sb("bl_bc", [P, D], F32)
        b_bc = sb("b_bc", [P, D], F32)

        edge = [sb("edge_src", [P, NT], I32), sb("edge_dst", [P, NT], I32)]
        shift_tail = sb("shift_tail", [1, 2, REST], I32)
        hi = [sb("hi_src", [P, NT], BF16), sb("hi_dst", [P, NT], BF16)]
        below = [sb("below_src", [P, NBX], F32), sb("below_dst", [P, NBX], F32)]
        sign_sum = sb("sign_sum", [P, NBX], F32)
        start = [sb("start_src", [P, NBX + 1], F32), sb("start_dst", [P, NBX + 1], F32)]
        unsorted = sb("unsorted", [P, 2], F32)
        unsorted_i = sb("unsorted_i", [1, 1], I32)
        base = sb("base", [P, NBX], F32)
        hot = sb("hot", [P, 2, K, NBX], BF16)
        rank_prod = sb("rank_prod", [P, K, NBX], F32)
        pos = sb("pos", [P, ROUND, K], I32)
        rec = sb("rec", [P, ROUND, K, 2], I32)

        start_i = sb("start_i", [P, NBX + 1], I32)
        first_i = sb("first_i", [P, NBX + 1], I32)
        first_f = sb("first_f", [P, NBX + 1], F32)
        last_i = sb("last_i", [P, NBX], I32)
        last_f = sb("last_f", [P, NBX], F32)
        npair = sb("npair", [P, NB], F32)
        pair_end = sb("pair_end", [P, NB], F32)
        shift_f = sb("shift_f", [P, NBX], F32)
        pick = sb("pick", [P, NBX], F32)
        pair_block = sb("pair_block", [P, NCH], F32)
        pair_block_i = sb("pair_block_i", [P, NCH], I32)
        pair_lo = sb("pair_lo", [P, NCH], F32)
        pair_row = sb("pair_row", [P, NCH], F32)
        pair_row_i = sb("pair_row_i", [P, NCH], I32)
        blocks = sb("blocks", [1, NPAIR], I32)
        list_row = sb("list_row", [P, 2, P, 2], I32)
        list_f = sb("list_f", [P, 2, P], F32)
        local = sb("local", [P, NPAIR], F32)
        other = sb("other", [P, NPAIR], I32)

        a_tab = sb("a_tab", [P, NBX * D], F32)
        acc = sb("acc", [P, NBX * SEG], F32)
        acc_col = acc[:, :].rearrange("p (n s) -> p n s", s=SEG)
        keyf = [acc[:, n * NT:(n + 1) * NT] for n in range(2)]
        unused = [acc[:, n * NT:(n + 1) * NT] for n in (2, 3)]
        stage = acc[:, 4 * NT:6 * NT].bitcast(I32).rearrange("p (c f) -> p c f", f=2)
        shifted = acc[:, 6 * NT:6 * NT + CW].bitcast(I32)
        xb = sb("xb", [P, D], F32)
        x_res = sb("x_res", [P, D], F32)
        xbT = sb("xbT", [P, D], F32)
        bx = sb("bx", [P, D], F32)
        idx = sb("idx", [P, ROUND, K], I32)
        got = sb("got", [P, ROUND, K, GW], F32)
        hot_e = sb("hot_e", [P, ROUND, K, P], BF16)
        hot_n = sb("hot_n", [P, 2, K, P], F32)
        hidden = sb("hidden", [P, 2, K, D], F32)
        logit = sb("logit", [P, 2, K], F32)
        weight = sb("weight", [P, 2, K], F32)
        whot = sb("whot", [P, 2, K, P], F32)
        done_by = sb("done_by", [P, 1], F32)
        turn_f = sb("turn_f", [1, NTICK - 1], F32)
        turn_skip = sb("turn_skip", [1, NTICK - 1], F32)
        turn_block = [sb(f"turn_block{n}", [1, NTICK - 1], I32) for n in range(2)]
        turn_store = [sb(f"turn_store{n}", [1, NTICK - 1], I32) for n in range(2)]
        late = sb("late", [1, 2], I32)
        seg_w = sb("seg_w", [P, 1], F32)
        seg_inv = sb("seg_inv", [P, 1], F32)
        has_edge = sb("has_edge", [P, 1], F32)
        keep_x = sb("keep_x", [P, 1], F32)
        scale = sb("scale", [P, 1], F32)
        emb_x = sb("emb_x", [P, D], F32)
        emb_e = sb("emb_e", [P, D], F32)
        embT = sb("embT", [P, D], F32)
        y = sb("y", [P, D], F32)
        result = sb("result", [P, D], F32)
        stats = sb("stats", [P, 6], F32)
        mv = sb("mv", [P, 2], F32)
        var_eps = sb("var_eps", [P, 1], F32)
        half_bits = sb("half_bits", [P, 1], I32)
        root = sb("root", [P, 1], F32)
        root_sq = sb("root_sq", [P, 1], F32)
        rstd = sb("rstd", [P, 1], F32)
        shift = sb("shift", [P, 1], F32)

        bank = [ctx.enter_context(nc.psum_tensor(f"bank{n}", [P, 512], F32)) for n in range(8)]
        bank_b = [t[:, 0:K * P // 2].bitcast(BF16) for t in bank]

        s_c = sem("constants")
        s_cv = sem("constants_vector")
        s_w = sem("weights_loaded")
        s_wt = sem("w_turned")
        s_wtc = sem("w_turned_copied")
        s_e = [sem("src_loaded"), sem("dst_loaded")]
        s_pad = sem("edge_padding")
        s_tab = sem("tables_filled")
        s_chain = sem("vector_chain")
        s_key = sem("keys_ready")
        s_thr = sem("sign_counts")
        s_bel = sem("below_counts")
        s_st = sem("starts_summed")
        s_start = sem("starts_ready")
        s_flag = sem("flag_ready")
        s_copy1 = sem("list1_written")
        s_list1 = sem("list1_ready")
        s_cnt1 = sem("dst_counted")
        s_cnt0 = sem("src_counted")
        s_done_by = sem("complete_blocks_counted")
        s_done_row = sem("complete_blocks_as_row")
        s_turns = sem("turns_ready")
        s_flag0 = sem("descents_counted")
        s_ac = sem("half_bounds_ready")
        s_idb = sem("ident_bf16_ready")

        class SortSems:
            def __init__(self, tag):
                self.hot = sem(f"{tag}_hot_ready")
                self.rank = sem(f"{tag}_rank_ready")
                self.base = sem(f"{tag}_base_ready")
                self.prod = sem(f"{tag}_prod_ready")
                self.pos = sem(f"{tag}_pos_ready")
                self.rec = sem(f"{tag}_records_ready")
                self.go = sem(f"{tag}_scatter_go")
                self.wrote = [sem(f"{tag}_scattered{n}") for n in range(ROUND)]

        sort0, sort1 = SortSems("sort0"), SortSems("sort1")

        s_xld = sem("x_block_loaded")
        s_xT = sem("x_turned")
        s_xTc = sem("x_turned_copied")
        s_ab = sem("ab_ready")
        s_aw = sem("a_written")
        s_bw = sem("b_written")
        s_bst = sem("b_stored")

        class PairSems:
            def __init__(self, tag):
                self.calc = sem(f"{tag}_pairs_ready")
                self.bst = sem(f"{tag}_blocks_stored")
                self.bld = sem(f"{tag}_blocks_loaded")
                self.got = [sem(f"{tag}_rows_gathered{n}") for n in range(2)]
                self.flt = sem(f"{tag}_rows_float")
                self.turn = sem(f"{tag}_rows_turned")
                self.done = sem(f"{tag}_columns_ready")

        pair0, pair1 = PairSems("pair0"), PairSems("pair1")

        class EdgeSems:
            def __init__(self, tag, attends):
                self.idx = sem(f"{tag}_idx_ready")
                self.go = sem(f"{tag}_gather_go")
                self.got = [sem(f"{tag}_gathered{n}") for n in range(ROUND)]
                self.hot = sem(f"{tag}_hot_ready")
                if attends:
                    self.turn = sem(f"{tag}_hot_turned")
                    self.turnc = sem(f"{tag}_hot_turned_copied")
                    self.a = sem(f"{tag}_a_spread")
                    self.hid = sem(f"{tag}_hidden_ready")
                    self.logit = sem(f"{tag}_logit_ready")
                    self.weight = sem(f"{tag}_weight_ready")
                    self.whot = sem(f"{tag}_weighted_hot_ready")
                self.sum = sem(f"{tag}_pair_summed")
                self.acc = sem(f"{tag}_pair_added")

        edge0, edge1 = EdgeSems("edge0", True), EdgeSems("edge1", False)

        class NodeSems:
            def __init__(self, tag):
                self.x = sem(f"{tag}_x_loaded")
                self.xres = sem(f"{tag}_residual_loaded")
                self.seg = sem(f"{tag}_sum_read")
                self.inv = sem(f"{tag}_sum_inverse_ready")
                self.fac = sem(f"{tag}_factors_ready")
                self.emb = sem(f"{tag}_emb_ready")
                self.turn = sem(f"{tag}_emb_turned")
                self.turnc = sem(f"{tag}_emb_turned_copied")
                self.lin = sem(f"{tag}_linear_ready")
                self.y = sem(f"{tag}_y_ready")
                self.st = sem(f"{tag}_stats_ready")
                self.go = sem(f"{tag}_aggregate_go")
                self.mv = sem(f"{tag}_meanvar_ready")
                self.root = sem(f"{tag}_root_steps")
                self.shift = sem(f"{tag}_shift_ready")
                self.res = sem(f"{tag}_result_ready")
                self.out = sem(f"{tag}_result_stored")

        node0, node1 = NodeSems("node0"), NodeSems("node1")

        def slot_use(r, lag=0):
            return (r + 1) * 16 * K

        def block_rows(table, nb, cols=None):
            view = table.rearrange("(n p) d -> n p d", p=P)
            return view[nb] if cols is None else view[nb, :, cols]

        SORT_LAG = 1
        EDGE_LAG = ROUND
        TURN_TAIL = range((NG + EDGE_LAG) // ROUND, NTICK + 2)
        TAIL_STEPS = len(TURN_TAIL) * ROUND

        def turn(r, lag):
            t = r - lag
            return None if isinstance(t, int) and not 0 <= t < NTICK else t

        def turn_is(eng, regs, table, t):
            if isinstance(t, int) and t == NTICK - 1:
                return NB - 1
            eng.load(regs, table[0:1, span(t, 1)])
            return eng.snap(regs[0], min_val=0, max_val=NB if any(table is t_ for t_ in turn_block) else NB - 2)

        def wait_again(eng, layer, s):
            flag_late = eng.value_load(late[0:1, layer:layer + 1], min_val=0, max_val=1)
            with eng.If(flag_late):
                eng.wait_ge(s.out, 16 * (NTICK + NB - 1))

        def all_blocks_again(eng, layer, body):
            flag_late = eng.value_load(late[0:1, layer:layer + 1], min_val=0, max_val=1)
            with eng.If(flag_late):
                with eng.Fori(0, NB - 1) as nb:
                    body(nb + NTICK, nb)
        SPLIT = 45

        block = ctx.enter_context(nc.Block())

        @block.sync
        def _(sp):
            flat = [v.rearrange("(p c) -> p c", c=CW) for v in (src[0:P * CW], dst[0:P * CW])]
            sp.wait_ge(s_pad, 2)
            for n, v in enumerate((src, dst)):
                sp.dma_start(edge[n][:, 0:CW], flat[n]).then_inc(s_e[n], 16)
                sp.dma_start(edge[n][0:REST, CW:CW + 1],
                             v[P * CW:E].rearrange("(p c) -> p c", c=1)).then_inc(s_e[n], 16)
            sp.dma_start(shifted[:, :], dst[1:P * CW + 1].rearrange("(p c) -> p c", c=CW)).then_inc(s_e[1], 16)
            sp.dma_start(shift_tail[:, 0, 0:REST - 1], dst[P * CW:E - 1].rearrange("(a c) -> a c", a=1)).then_inc(s_e[1], 16)
            sp.dma_start(shift_tail[:, 1, 0:REST - 1], dst[P * CW + 1:E].rearrange("(a c) -> a c", a=1)).then_inc(s_e[1], 16)
            sp.dma_start(table0[0:N, D:2 * D], x).then_inc(s_tab, 16)
            sp.wait_ge(s_cv, 1)
            pad = ROWS - N
            sp.dma_start(table0[N:N + P, D:2 * D], zeros[:, 0:D]).then_inc(s_tab, 16)
            sp.dma_start(table0[N + P:ROWS, D:2 * D], zeros[0:pad - P, 0:D]).then_inc(s_tab, 16)
            sp.dma_start(block_rows(table0, NB, slice(0, D)), zeros[:, 0:D]).then_inc(s_tab, 16)
            sp.dma_start(block_rows(table1, NB), zeros[:, 0:D]).then_inc(s_tab, 16)
            sp.dma_start(w1[:, :, :], W1.rearrange("(t p) d -> p t d", p=P)).then_inc(s_w, 16)
            sp.dma_start(w2[:, :], W2.rearrange("d a -> a d").to_broadcast([P, D])).then_inc(s_w, 16)
            sp.dma_start(wl[:, :], Wl).then_inc(s_w, 16)
            sp.dma_start(w_in[:, :], W).then_inc(s_w, 16)
            for tile, v in ((b1_bc, b1), (bl_bc, bl), (b_bc, b), (b2_bc, b2)):
                sp.dma_start(tile[:, :], v.rearrange("(a d) -> a d", a=1).to_broadcast([P, v.shape[0]])).then_inc(s_w, 16)

            sp.wait_ge(s_copy1, 2)
            view = lists[1].rearrange("t (p c) -> (t p) c", c=2)
            sp.dma_start(view[0:P * CW, :].rearrange("(p c) f -> p (c f)", c=CW),
                         stage[:, 0:CW, :].rearrange("p c f -> p (c f)")).then_inc(s_list1, 16)
            sp.dma_start(view[P * CW:P * (CW + 1), :], stage[:, CW, :]).then_inc(s_list1, 16)

            sp.wait_ge(s_tab, 80)
            sp.dma_start(xb[:, :], block_rows(table0, 0, slice(D, 2 * D))).then_inc(s_xld, 16)
            with sp.Fori(1, NB) as nb:
                sp.wait_ge(s_xT, nb)
                sp.dma_start(xb[:, :], block_rows(table0, nb, slice(D, 2 * D))).then_inc(s_xld, 16)
                sp.wait_ge(s_bw, nb)
                sp.dma_start(block_rows(table0, nb - 1, slice(0, D)), bx[:, :]).then_inc(s_bst, 16)
            sp.wait_ge(s_bw, NB)
            sp.dma_start(block_rows(table0, NB - 1, slice(0, D)), bx[:, :]).then_inc(s_bst, 16)

            def pair_blocks(s, n):
                sp.wait_ge(s.calc, 1)
                with nc.allow_non_contiguous_dma(reason="13 columns of block numbers"):
                    sp.dma_start(blocks_dram[n].rearrange("c p -> p c"), pair_block_i[:, :]).then_inc(s.bst, 16)
                sp.wait_ge(s.bst, 16)
                sp.dma_start(blocks[:, :], blocks_dram[n].rearrange("(a c) p -> a (c p)", a=1)).then_inc(s.bld, 16)

            regs = [sp.alloc_register("sp_block")]

            def load_x(s, table, cols, t, nb):
                wait(sp, s.emb, t)
                sp.dma_start(xb[:, :], block_rows(table, nb, cols)).then_inc(s.x, 16)

            def load_residual(s, table, cols, t, nb):
                wait(sp, s.y, t)
                sp.dma_start(x_res[:, :], block_rows(table, nb, cols)).then_inc(s.xres, 16)

            def store(s, target, last_rows, t, nb):
                sp.wait_ge(s.res, t + 1)
                if isinstance(nb, int) and nb == NB - 1:
                    sp.dma_start(target[nb * P:nb * P + last_rows, :], result[0:last_rows, :]).then_inc(s.out, 16)
                else:
                    view = target[0:(NB - 1) * P, :].rearrange("(n p) d -> n p d", p=P)
                    sp.dma_start(view[nb], result[:, :]).then_inc(s.out, 16)

            def node_io(s, layer, table, cols, target, last_rows):
                def step(r, j):
                    t = turn(r, 1)
                    if t is not None:
                        load_residual(s, table, cols, t, turn_is(sp, regs, turn_block[layer], t))
                    t = turn(r, 0)
                    if t is not None and layer == 0:
                        load_x(s, table, cols, t, turn_is(sp, regs, turn_block[layer], t))
                    t = turn(r, 2)
                    if t is not None:
                        store(s, target, last_rows, t, turn_is(sp, regs, turn_store[layer], t))

                def again(t, nb):
                    if layer == 0:
                        load_x(s, table, cols, t, nb)
                    load_residual(s, table, cols, t, nb)
                    store(s, target, last_rows, t, nb)

                run_steps(sp, NG // ROUND, EDGE_LAG // ROUND, step, 1)
                if layer == 0:
                    pair_blocks(pair1, 1)
                for r in TURN_TAIL:
                    step(r, 0)
                sp.wait_ge(s.out, 16 * NTICK)
                all_blocks_again(sp, layer, again)

            pair_blocks(pair0, 0)
            sp.wait_ge(s_xT, NB)
            sp.wait_ge(s_turns, 1)
            node_io(node0, 0, table0, slice(D, 2 * D), table1, P)
            sp.wait_ge(node0.out, 16 * NTICK)
            wait_again(sp, 0, node0)
            sp.wait_ge(s_turns, 2)
            node_io(node1, 1, table1, slice(0, D), out, TAIL)
            wait_again(sp, 1, node1)

        @block.gpsimd
        def _(pool):
            def ramp(tile, step, n, partition, base=0):
                pool.iota(tile[:, :], [[step, n]], base=base, channel_multiplier=partition,
                          allow_small_or_imprecise_dtypes=True).then_inc(s_c, 1)

            ramp(bound_f, P, NBX, 0)
            ramp(iota_f, 1, P, 0)
            ramp(iota_b, 1, P, 0)
            ramp(pair_no, P, NCH, 1)
            ramp(turn_no, 2 * K, 2, ROUND * K)
            pool.wait_ge(s_cv, 3)
            pool.affine_select(out=ident[:, :], in_=zeros[:, 0:P], compare_op=ALU.not_equal, fill=1.0, base=0,
                               pattern=[[-1, P]], channel_multiplier=1).then_inc(s_c, 1)
            pool.affine_select(out=upper_b[:, :], in_=ones_b[:, :], compare_op=ALU.is_gt, fill=0.0, base=0,
                               pattern=[[1, P]], channel_multiplier=-1).then_inc(s_c, 1)

            def scatter(s, n):
                target = lists[n].rearrange("t (p c) -> (t p) c", c=2)
                def step(r, j):
                    q = r * ROUND + j
                    pool.wait_ge(s.pos, q + 1)
                    pool.wait_ge(s.rec, q + 1)
                    pool.sem_inc(s.go, 1)
                    for k in range(K):
                        pool.indirect_dma_start(target, bass.IndirectOffsetOnAxis(pos[:, j, k:k + 1], 0),
                                                rec[:, j, k, :], None).then_inc(s.wrote[j], 16)
                run_steps(pool, NQ, 0, step)
                for j in range(ROUND):
                    pool.wait_ge(s.wrote[j], slot_use(ROUNDS_SORT - 1))

            def gather_rows(s, n):
                pool.wait_ge(s.calc, 1)
                for c in range(NCH):
                    if c >= 2:
                        pool.wait_ge(s.flt, 2 * (c - 1))
                    pool.indirect_dma_start(list_row[:, c % 2, :, :].rearrange("p e f -> p (e f)"), None, lists[n],
                                            bass.IndirectOffsetOnAxis(pair_row_i[:, c:c + 1], 0)).then_inc(s.got[c % 2], 16)

            def gather_edges(s, table, width):
                def step(r, j):
                    pool.wait_ge(s.idx, r * ROUND + j + 1)
                    pool.sem_inc(s.go, 1)
                    for k in range(K):
                        off = 2 * D - width
                        pool.indirect_dma_start(got[:, j, k, off:off + width], None, table,
                                                bass.IndirectOffsetOnAxis(idx[:, j, k:k + 1], 0)).then_inc(s.got[j], 16)
                run_steps(pool, NG, 0, step)

            scatter(sort0, 0)
            gather_rows(pair0, 0)
            pool.wait_ge(s_bst, 16 * NB)
            gather_edges(edge0, table0, 2 * D)
            pool.wait_ge(s_flag, 1)
            pool.wait_ge(s_list1, 32)
            flag = pool.value_load(unsorted_i[0:1, 0:1], min_val=0, max_val=1)
            with pool.If(flag):
                scatter(sort1, 1)
            gather_rows(pair1, 1)
            pool.wait_ge(node0.out, 16 * NTICK)
            wait_again(pool, 0, node0)
            gather_edges(edge1, table1, D)

        @block.scalar
        def _(act):
            act.wait_ge(s_c, 1)
            act.activation(bound_h[:, :], bound_f[:, :], ACT.Copy, bias=-0.5).then_inc(s_ac, 1)
            act.wait_ge(s_ac, 1)
            act.wait_ge(s_key, 1)
            act.activation(unused[1], keyf[0], ACT.Sign, bias=bound_h[:, SPLIT:SPLIT + 1], scale=-1.0,
                           accum_out=sign_sum[:, SPLIT:SPLIT + 1]).then_inc(s_thr, 1)
            with act.Fori(SPLIT + 1, NBX) as nb:
                act.wait_ge(s_thr, nb - SPLIT)
                act.activation(unused[1], keyf[0], ACT.Sign, bias=bound_h[:, bass.ds(nb, 1)], scale=-1.0,
                               accum_out=sign_sum[:, bass.ds(nb, 1)]).then_inc(s_thr, 1)

            def sort_side(s, with_blocks):
                def step(r, j):
                    q = r * ROUND + j
                    if not (isinstance(r, int) and r < 1):
                        act.wait_ge(s.wrote[j], slot_use(r - 1))
                    for f in range(2):
                        act.copy(rec[:, j, :, f], edge[f][:, span(q * K, K)]).then_inc(s.rec, 1)
                    act.wait_ge(s.rank, q + 1)
                    act.wait_ge(s.base, q + 1)
                    act.copy(base[:, :], bank[j % 2][:, K * NBX:(K + 1) * NBX]).then_inc(s.base, 1)
                    if with_blocks and j == 0:
                        act.wait_ge(s_xT, r + 1)
                        wait(act, s_ab, r)
                        act.copy(xbT[:, :], bank[2][:, 0:P]).then_inc(s_xTc, 1)
                    if with_blocks and j == 2:
                        act.wait_ge(s_ab, r + 1)
                        wait(act, s_bst, 16 * r)
                        act.copy(bx[:, :], bank[4][:, 0:D]).then_inc(s_bw, 1)
                run_steps(act, NQ, 0, step)

            def pair_columns(s, c):
                act.wait_ge(s.turn, c + 1)
                act.copy(local[:, c * P:(c + 1) * P], bank[6][:, 0:P]).then_inc(s.done, 1)
                act.copy(other[:, c * P:(c + 1) * P], bank[6][:, P:2 * P]).then_inc(s.done, 1)

            def indices(s, r, j):
                at = back(r, j, 0, NG)
                if at is not None:
                    g = at[2]
                    wait(act, s.sum, HALVES * (g - ROUND + 1))
                    act.copy(idx[:, j, :], other[:, span(g * K, K)]).then_inc(s.idx, 1)

            def copy_turned(s, t):
                act.wait_ge(s.turn, t + 1)
                wait(act, s.lin, t)
                act.copy(embT[:, :], bank[0][:, 2 * P:3 * P]).then_inc(s.turnc, 1)

            def embed(s, layer, t, nb):
                edges = nb * SEG + (D + 1, D)[layer]
                act.wait_ge(s.inv, t + 1)
                act.activation(has_edge[:, :], acc[:, span(edges, 1)], ACT.Sign).then_inc(s.fac, 1)
                act.wait_ge(s.fac, t * (3 - layer) + 1)
                act.activation(scale[:, :], seg_inv[:, :], ACT.Copy, scale=has_edge[:, :]).then_inc(s.fac, 1)
                if layer == 0:
                    act.activation(keep_x[:, :], has_edge[:, :], ACT.Copy, scale=-0.5, bias=1.0).then_inc(s.fac, 1)
                wait(act, s.turn, t)
                act.wait_ge(s.fac, t * (3 - layer) + 3 - layer)
                if layer == 0:
                    act.activation(emb_e[:, :], acc[:, span(nb * SEG, D)], ACT.Copy, scale=scale[:, :])
                    act.wait_ge(s.x, 16 * (t + 1))
                    act.activation(emb_x[:, :], xb[:, :], ACT.Copy, scale=keep_x[:, :]).then_inc(s.emb, 1)
                else:
                    act.activation(emb_e[:, :], acc[:, span(nb * SEG, D)], ACT.Copy, scale=scale[:, :]).then_inc(s.emb, 1)

            def normalise(s, t):
                act.wait_ge(s.shift, t + 1)
                wait(act, s.out, 16 * t)
                act.activation(result[:, :], y[:, :], ACT.Identity, scale=rstd[:, :], bias=shift[:, :]).then_inc(s.res, 1)

            regs = [act.alloc_register("act_block")]

            def turn_step(s, layer, r, j):
                t = turn(r, 1)
                if t is not None and j == 2:
                    copy_turned(s, t)

            def turn_middle(s, layer, r, j):
                t = turn(r, 1)
                if t is not None and j == 1:
                    embed(s, layer, t, turn_is(act, regs, turn_block[layer], t))

            def turn_late(s, layer, r, j):
                t = turn(r, 2)
                if t is not None and j == 3:
                    normalise(s, t)

            def again(s, layer):
                def body(t, nb):
                    embed(s, layer, t, nb)
                    copy_turned(s, t)
                    normalise(s, t)
                return body

            def edge0_step(r, j):
                indices(edge0, r, j)
                at = back(r, j, 0, NG)
                if at is not None:
                    act.wait_ge(edge0.turn, at[2] + 1)
                turn_step(node0, 0, r, j)
                if at is not None:
                    g = at[2]
                    wait(act, edge0.a, g - 1)
                    act.copy(hot_n[:, j % 2, :, :].rearrange("p k n -> p (k n)"), bank_b[j % 2]).then_inc(edge0.turnc, 1)
                turn_middle(node0, 0, r, j)
                at = back(r, j, 2, NG)
                if at is not None:
                    _, jj, g = at
                    act.wait_ge(edge0.logit, g + 1)
                    act.activation(weight[:, jj % 2, :], logit[:, jj % 2, :], ACT.Sigmoid, bias=b2_bc[:, :]).then_inc(edge0.weight, 1)
                    act.wait_ge(edge0.weight, g + 1)
                    wait(act, edge0.sum, HALVES * (g - 1))
                    for k in range(K):
                        last = act.activation(whot[:, jj % 2, k, :], hot_e[:, jj, k, :], ACT.Copy,
                                              scale=weight[:, jj % 2, k:k + 1])
                    last.then_inc(edge0.whot, 1)
                turn_late(node0, 0, r, j)

            def edge1_step(r, j):
                indices(edge1, r, j)
                turn_step(node1, 1, r, j)
                turn_middle(node1, 1, r, j)
                turn_late(node1, 1, r, j)

            for n in range(2):
                act.wait_ge(s_e[n], (32, 80)[n])
            sort_side(sort0, True)
            for c in range(NCH):
                pair_columns(pair0, c)
            act.wait_ge(s_w, 16 * 8)
            run_steps(act, NG, EDGE_LAG, edge0_step)
            act.wait_ge(s_flag, 1)
            flag = act.value_load(unsorted_i[0:1, 0:1], min_val=0, max_val=1)
            with act.If(flag):
                for j in range(ROUND):
                    act.wait_ge(sort0.wrote[j], slot_use(ROUNDS_SORT - 1))
                sort_side(sort1, False)
            act.wait_ge(edge0.sum, HALVES * NG)
            for c in range(NCH - TAIL_STEPS):
                pair_columns(pair1, c)
            for r in TURN_TAIL:
                for j in range(ROUND):
                    c = (r - TURN_TAIL[0]) * ROUND + j + NCH - TAIL_STEPS
                    if 0 <= c < NCH:
                        pair_columns(pair1, c)
                    turn_step(node0, 0, r, j)
                    turn_middle(node0, 0, r, j)
                    turn_late(node0, 0, r, j)
            all_blocks_again(act, 0, again(node0, 0))
            run_steps(act, NG, EDGE_LAG, edge1_step)
            for r in TURN_TAIL:
                for j in range(ROUND):
                    turn_step(node1, 1, r, j)
                    turn_middle(node1, 1, r, j)
                    turn_late(node1, 1, r, j)
            all_blocks_again(act, 1, again(node1, 1))

        @block.tensor
        def _(pe):
            regs = [pe.alloc_register(f"pe_block{k}") for k in range(K)]

            pe.wait_ge(s_cv, 3)
            pe.wait_ge(s_c, 7)
            pe.wait_ge(s_idb, 1)
            pe.wait_ge(s_bel, 1)
            pe.matmul(bank[0][:, 0:NBX], ones[:, :], below[0][:, :], start=True, stop=True).then_inc(s_st, 1)
            pe.wait_ge(s_flag0, 1)
            pe.matmul(bank[1][:, 0:2], ones[:, :], unsorted[:, :], start=True, stop=True).then_inc(s_st, 1)
            pe.wait_ge(s_w, 16 * 8)
            pe.transpose(bank[2][:, 0:P], w_in[:, :], ident[:, :]).then_inc(s_wt, 1)
            pe.wait_ge(s_wtc, 1)

            def ranks(s, with_blocks):
                def step(r, j):
                    q = r * ROUND + j
                    view = bank[j % 2][:, 0:(K + 1) * NBX].rearrange("p (k n) -> p k n", n=NBX)
                    pe.wait_ge(s.hot, q + 1)
                    pe.wait_ge(s.base, q + 1)
                    wait(pe, s.prod, q - 1)
                    pe.matmul(view, ident[:, :], base[:, :].rearrange("p (a n) -> p a n", a=1).to_broadcast([P, K + 1, NBX]),
                              start=True, stop=False)
                    pe.matmul(view[:, 0:K, :], upper_b[:, :], hot[:, j % 2, :, :], start=False, stop=False)
                    for k in range(K):
                        last = pe.matmul(view[:, k + 1:K + 1, :], ones_b[:, :],
                                         hot[:, j % 2, k:k + 1, :].to_broadcast([P, K - k, NBX]),
                                         start=False, stop=(k == K - 1))
                    last.then_inc(s.rank, 1)
                    if with_blocks and j == 0:
                        pe.wait_ge(s_xld, 16 * (r + 1))
                        wait(pe, s_xTc, r)
                        pe.transpose(bank[2][:, 0:P], xb[:, :], ident[:, :]).then_inc(s_xT, 1)
                    if with_blocks and j == 1:
                        pe.wait_ge(s_xTc, r + 1)
                        wait(pe, s_aw, r)
                        pe.matmul(bank[3][:, 0:D], xbT[:, :], w1[:, 0, :], start=True, stop=True)
                        wait(pe, s_bw, r)
                        pe.matmul(bank[4][:, 0:D], xbT[:, :], w1[:, 1, :], start=True, stop=True).then_inc(s_ab, 1)
                run_steps(pe, NQ, 0, step)

            def turn_rows(s, c):
                pe.wait_ge(s.flt, 2 * (c + 1))
                if c:
                    pe.wait_ge(s.done, 2 * c)
                pe.transpose(bank[6][:, 0:P], list_f[:, 0, :], ident[:, :])
                pe.transpose(bank[6][:, P:2 * P], list_f[:, 1, :], ident[:, :]).then_inc(s.turn, 1)

            def complete_row(n):
                pe.wait_ge(s_done_by, n + 1)
                pe.matmul(bank[7][0:1, 0:P], done_by[:, :], ident[:, :], start=True, stop=True).then_inc(s_done_row, 1)

            def turn_emb(s, layer, t):
                pe.wait_ge(s.emb, t + 1)
                wait(pe, s.turnc, t)
                area = bank[0][:, 2 * P:3 * P]
                if layer == 0:
                    pe.matmul(area, emb_x[:, :], ident[:, :], start=True, stop=False)
                    pe.matmul(area, emb_e[:, :], ident[:, :], start=False, stop=True).then_inc(s.turn, 1)
                else:
                    pe.transpose(area, emb_e[:, :], ident[:, :]).then_inc(s.turn, 1)

            def linear(s, layer, t):
                pe.wait_ge(s.turnc, t + 1)
                wait(pe, s.y, t)
                area = bank[4][:, LIN_AT:LIN_AT + D]
                pe.matmul(area, embT[:, :], (wl, wt)[layer][:, :], start=True, stop=False)
                pe.matmul(area, ones[0:1, :], (bl_bc, b_bc)[layer][0:1, :], start=False, stop=True).then_inc(s.lin, 1)

            def turn_step(s, layer, r, j):
                t = turn(r, 1)
                if t is not None and j == 2:
                    turn_emb(s, layer, t)
                if t is not None and j == 3:
                    linear(s, layer, t)

            def again(s, layer):
                def body(t, nb):
                    turn_emb(s, layer, t)
                    linear(s, layer, t)
                return body

            def in_bank4(s, layer, r, j):
                if j == 3:
                    turn_step(s, layer, r, 3)
                if j == 1 and turn(r, 2) is not None:
                    pe.wait_ge(s.y, turn(r, 2) + 1)

            def sums(s, r, j, lag, lhs, count, shared):
                at = back(r, j, lag, NG)
                if at is None:
                    if r > 0:
                        pe.wait_ge(s.acc, NPAIR)
                    shared()
                    return
                rr, jj, g = at
                pe.wait_ge(s.got[jj], slot_use(rr))
                for k in range(K):
                    h, i = k // (K // HALVES), k % (K // HALVES)
                    if i == 0:
                        wait(pe, s.acc, K * (g - 2) + (h + 1) * (K // HALVES))
                    if k == 0:
                        shared()
                    area = bank[4 + HALVES * (jj % 2) + h][:, i * SEG:(i + 1) * SEG]
                    last = pe.matmul(area[:, 0:D + 1], lhs(jj, k), got[:, jj, k, D:2 * D + 1], start=True, stop=True)
                    if count:
                        last = pe.matmul(area[:, D + 1:D + 2], hot_e[:, jj, k, :], ones_b[:, 0:1], start=True, stop=True)
                    if i == K // HALVES - 1:
                        last.then_inc(s.sum, 1)

            def edge0_step(r, j):
                at = back(r, j, 1, NG)
                if at is not None:
                    _, jj, g = at
                    pe.load(regs, blocks[0:1, span(g * K, K)])
                    nbs = [pe.snap(v, min_val=0, max_val=NB) for v in regs]
                    pe.wait_ge(edge0.turnc, g + 1)
                    wait(pe, edge0.hid, g - 1)
                    for k in range(K):
                        last = pe.matmul(bank[2 + jj % 2][:, k * D:(k + 1) * D], hot_n[:, jj % 2, k, :],
                                         a_tab[:, bass.ds(nbs[k] * D, D)], start=True, stop=True)
                    last.then_inc(edge0.a, 1)
                at = back(r, j, 0, NG)
                if at is not None:
                    g = at[2]
                    wait(pe, edge0.turnc, g - 1)
                if j == 2:
                    turn_step(node0, 0, r, 2)
                if at is not None:
                    pe.wait_ge(edge0.hot, g + 1)
                    for k in range(K):
                        last = pe.transpose(bank_b[j % 2][:, k * P:(k + 1) * P], hot_e[:, j, k, :], ident_b[:, :])
                    last.then_inc(edge0.turn, 1)
                at = back(r, j, 3, NG)
                if at is not None:
                    pe.wait_ge(edge0.whot, at[2] + 1)
                sums(edge0, r, j, 3, lambda jj, k: whot[:, jj % 2, k, :], True, lambda: in_bank4(node0, 0, r, j))

            def edge1_step(r, j):
                at = back(r, j, 1, NG)
                if at is not None:
                    pe.wait_ge(edge1.hot, at[2] + 1)
                sums(edge1, r, j, 1, lambda jj, k: whot[:, jj % 2, k, :], False, lambda: in_bank4(node1, 1, r, j))
                if j == 2:
                    turn_step(node1, 1, r, 2)

            pe.wait_ge(sort0.base, 1)
            pe.wait_ge(s_flag, 1)
            ranks(sort0, True)
            pe.wait_ge(s_bel, 2)
            pe.wait_ge(s_aw, NB)
            pe.matmul(bank[3][:, 0:NBX], ones[:, :], below[1][:, :], start=True, stop=True).then_inc(s_st, 1)
            pe.wait_ge(s_bw, NB)
            complete_row(0)
            for c in range(NCH):
                turn_rows(pair0, c)
            pe.wait_ge(pair0.bld, 16)
            run_steps(pe, NG, EDGE_LAG, edge0_step)
            flag = pe.value_load(unsorted_i[0:1, 0:1], min_val=0, max_val=1)
            with pe.If(flag):
                ranks(sort1, False)
            complete_row(1)
            for c in range(NCH - TAIL_STEPS):
                turn_rows(pair1, c)
            for r in TURN_TAIL:
                for j in range(ROUND):
                    c = (r - TURN_TAIL[0]) * ROUND + j + NCH - TAIL_STEPS
                    if 0 <= c < NCH:
                        turn_rows(pair1, c)
                    turn_step(node0, 0, r, j)
            all_blocks_again(pe, 0, again(node0, 0))
            run_steps(pe, NG, EDGE_LAG, edge1_step)
            for r in TURN_TAIL:
                for j in range(ROUND):
                    turn_step(node1, 1, r, j)
            all_blocks_again(pe, 1, again(node1, 1))

        @block.vector
        def _(v):
            regs = [v.alloc_register(f"v_block{k}") for k in range(K)]
            turn_regs = [v.alloc_register("v_turn_block")]
            links = 0

            def link(ins):
                nonlocal links
                links += 1
                ins.then_inc(s_chain, 1)
                v.wait_ge(s_chain, links)

            for n in range(2):
                v.memset(edge[n][:, CW:NT], PAD_KEY).then_inc(s_pad, 1)
            v.memset(zeros[:, :], 0.0).then_inc(s_cv, 1)
            v.memset(ones[:, :], 1.0).then_inc(s_cv, 1)
            v.memset(ones_b[:, :], 1.0).then_inc(s_cv, 1)
            v.memset(got[:, :, :, 2 * D:2 * D + 1], 1.0)
            v.memset(a_tab[:, NB * D:NBX * D], 0.0)
            link(v.memset(unsorted[:, :], 0.0))

            for n in range(2):
                v.wait_ge(s_e[n], (32, 80)[n])
                v.tensor_copy(keyf[n], edge[n][:, :]).then_inc(s_key, 1)
                link(v.tensor_scalar(other[:, 0:NT], edge[n][:, :], 7, None, ALU.arith_shift_right))
                link(v.tensor_copy(hi[n][:, :], other[:, 0:NT]))
            v.wait_ge(s_c, 7)
            v.tensor_copy(ident_b[:, :], ident[:, :]).then_inc(s_idb, 1)

            def count(n, nb):
                return v.tensor_scalar(unused[0], keyf[n], bound_f[:, span(nb, 1)], None, ALU.is_lt, ALU.add,
                                       accum_out=below[n][:, span(nb, 1)])

            count(0, 0).then_inc(s_cnt0, 1)
            with v.Fori(1, SPLIT) as nb:
                v.wait_ge(s_cnt0, nb)
                count(0, nb).then_inc(s_cnt0, 1)
            v.wait_ge(s_cnt0, SPLIT)
            v.wait_ge(s_thr, NBX - SPLIT)
            v.tensor_scalar(below[0][:, SPLIT:NBX], sign_sum[:, SPLIT:NBX], 0.5, NT / 2, ALU.mult, ALU.add).then_inc(s_bel, 1)
            link(v.scalar_tensor_tensor(out=unused[0][:, 0:CW], in0=shifted, scalar=0.0, in1=edge[1][:, 0:CW],
                                        op0=ALU.add, op1=ALU.is_lt, accum_out=unsorted[:, 0:1]))
            v.scalar_tensor_tensor(out=unused[0][0:1, 0:REST - 1], in0=shift_tail[:, 1, 0:REST - 1], scalar=0.0,
                                   in1=shift_tail[:, 0, 0:REST - 1], op0=ALU.add, op1=ALU.is_lt,
                                   accum_out=unsorted[0:1, 1:2]).then_inc(s_flag0, 1)
            v.wait_ge(s_st, 1)
            v.tensor_copy(start[0][:, 0:NBX], bank[0][:, 0:NBX])
            v.tensor_copy(base[:, :], bank[0][:, 0:NBX]).then_inc(sort0.base, 1)
            v.wait_ge(s_st, 2)
            link(v.tensor_reduce(unsorted[:, 0:1], bank[1][:, 0:2], AX_X, ALU.add))
            v.tensor_scalar(unsorted_i[:, :], unsorted[0:1, 0:1], 1.0, None, ALU.min).then_inc(s_flag, 1)
            for f in range(2):
                v.tensor_copy(stage[:, :, f], edge[f][:, :]).then_inc(s_copy1, 1)
            v.wait_ge(s_wt, 1)
            v.tensor_copy(wt[:, :], bank[2][:, 0:P]).then_inc(s_wtc, 1)
            v.wait_ge(s_w, 16 * 8)

            def places(s, n, with_blocks):
                def step(r, j):
                    at = back(r, j, 0, NQ)
                    if at is not None:
                        q = at[2]
                        wait(v, s.rank, q - 1)
                        wait(v, s.prod, q - 1)
                        v.tensor_tensor(hot[:, j % 2, :, :],
                                        hi[n][:, span(q * K, K)].rearrange("p (k a) -> p k a", a=1).to_broadcast([P, K, NBX]),
                                        iota_b[:, 0:NBX].rearrange("p (a n) -> p a n", a=1).to_broadcast([P, K, NBX]),
                                        ALU.is_equal).then_inc(s.hot, 1)
                    at = back(r, j, 1, NQ)
                    if at is not None:
                        rr, jj, q = at
                        v.wait_ge(s.base, q + 2)
                        wait(v, s.pos, q)
                        v.tensor_tensor(rank_prod[:, :, :], hot[:, jj % 2, :, :],
                                        bank[jj % 2][:, 0:K * NBX].rearrange("p (k n) -> p k n", n=NBX),
                                        ALU.mult).then_inc(s.prod, 1)
                        if with_blocks and j == 2:
                            v.wait_ge(s_ab, r + 1)
                            v.tensor_tensor(a_tab[:, span(r * D, D)], bank[3][:, 0:D], b1_bc[:, :], ALU.add).then_inc(s_aw, 1)
                        if with_blocks and j == 3:
                            wait(v, s_cnt1, r)
                            count(1, r).then_inc(s_cnt1, 1)
                        v.wait_ge(s.prod, q + 1)
                        if not (isinstance(rr, int) and rr < 1):
                            v.wait_ge(s.wrote[jj], slot_use(rr - 1))
                        with nc.allow_low_precision(reason="places are whole numbers below 2 ** 24"):
                            v.tensor_reduce(pos[:, jj, :], rank_prod[:, :, :], AX_X, ALU.add).then_inc(s.pos, 1)
                run_steps(v, NQ, SORT_LAG, step)

            def pairs(s, n):
                st = start[n]
                link(v.tensor_copy(start_i[:, 0:NBX], st[:, 0:NBX]))
                link(v.tensor_scalar(first_i[:, 0:NBX], start_i[:, 0:NBX], 7, None, ALU.arith_shift_right))
                link(v.tensor_copy(first_f[:, 0:NBX], first_i[:, 0:NBX]))
                link(v.tensor_scalar(start_i[:, 0:NB], st[:, 1:NBX], -1.0, None, ALU.add))
                link(v.tensor_scalar(last_i[:, 0:NB], start_i[:, 0:NB], 7, None, ALU.arith_shift_right))
                link(v.tensor_copy(last_f[:, 0:NB], last_i[:, 0:NB]))
                link(v.tensor_tensor(last_f[:, 0:NB], last_f[:, 0:NB], first_f[:, 0:NB], ALU.subtract))
                link(v.tensor_tensor(pick[:, 0:NB], st[:, 1:NBX], st[:, 0:NB], ALU.is_gt))
                link(v.scalar_tensor_tensor(out=npair[:, :], in0=last_f[:, 0:NB], scalar=1.0, in1=pick[:, 0:NB],
                                            op0=ALU.add, op1=ALU.mult))
                link(v.tensor_tensor_scan(pair_end[:, :], npair[:, :], zeros[:, 0:NB], 0.0, ALU.add, ALU.add))
                link(v.memset(shift_f[:, :], -4.0 * NPAIR))
                link(v.tensor_tensor(shift_f[:, 0:NB], first_f[:, 0:NB], pair_end[:, :], ALU.subtract))
                link(v.tensor_tensor(shift_f[:, 0:NB], shift_f[:, 0:NB], npair[:, :], ALU.add))
                for c in range(NCH):
                    link(v.tensor_scalar(pick[:, 0:NB], pair_end[:, :], pair_no[:, c:c + 1], None, ALU.is_le, ALU.add,
                                         accum_out=pair_block[:, c:c + 1]))
                    link(v.scalar_tensor_tensor(out=pick[:, :], in0=iota_f[:, 0:NBX], scalar=pair_block[:, c:c + 1],
                                                in1=shift_f[:, :], op0=ALU.is_equal, op1=ALU.mult,
                                                accum_out=pair_row[:, c:c + 1]))
                link(v.tensor_tensor(pair_row[:, :], pair_row[:, :], pair_no[:, :], ALU.add))
                link(v.tensor_scalar(pair_row[:, :], pair_row[:, :], 0.0, REAL_ROWS - 1.0, ALU.max, ALU.min))
                v.tensor_scalar(pick[:, 0:NB - 1], pair_end[:, 0:NB - 1], turn_no[:, n:n + 1], None, ALU.is_le, ALU.add,
                                accum_out=done_by[:, :]).then_inc(s_done_by, 1)
                v.tensor_copy(pair_row_i[:, :], pair_row[:, :])
                v.tensor_scalar(pair_lo[:, :], pair_block[:, :], float(P), None, ALU.mult)
                v.tensor_copy(pair_block_i[:, :], pair_block[:, :]).then_inc(s.calc, 1)
                v.wait_ge(s.calc, 1)

            def turns(n):
                v.wait_ge(s_done_row, n + 1)
                link(v.tensor_scalar(turn_f[:, :], bank[7][0:1, 0:NTICK - 1], -1.0, None, ALU.add))
                link(v.tensor_tensor_scan(turn_f[:, :], ones[0:1, 0:NTICK - 1], turn_f[:, :], -1.0, ALU.add, ALU.min))
                link(v.tensor_scalar(turn_skip[:, :], turn_f[:, :], 0.0, NB + 1.0, ALU.is_lt, ALU.mult))
                v.tensor_tensor(turn_block[n][:, :], turn_f[:, :], turn_skip[:, :], ALU.add)
                v.tensor_scalar(turn_store[n][:, :], turn_f[:, :], 0.0, None, ALU.max)
                v.tensor_scalar(late[:, n:n + 1], turn_f[:, NTICK - 2:NTICK - 1], NB - 2.0, None, ALU.is_lt).then_inc(s_turns, 1)

            def rows_float(s, field, c):
                v.wait_ge(s.got[c % 2], 16 * (c // 2 + 1))
                if c:
                    v.wait_ge(s.turn, c)
                v.tensor_scalar(list_f[:, 0, :], list_row[:, c % 2, :, field], pair_lo[:, c:c + 1], None,
                                ALU.subtract).then_inc(s.flt, 1)
                v.tensor_copy(list_f[:, 1, :], list_row[:, c % 2, :, 1 - field]).then_inc(s.flt, 1)

            def one_hots(s, r, j, out, free):
                at = back(r, j, 0, NG)
                if at is not None:
                    g = at[2]
                    wait(v, s.sum, HALVES * (g - free + 1))
                    for k in range(K):
                        last = v.tensor_scalar(out(k), iota_b[:, :], local[:, span(g * K + k, 1)], None, ALU.is_equal)
                    last.then_inc(s.hot, 1)

            def add_sums(s, r, j, lag, cols, between, leave):
                at = back(r, j, lag, NG)
                if at is not None:
                    g = at[2]
                    v.load(regs, blocks[0:1, span(g * K, K)])
                    nbs = [v.snap(x_, min_val=0, max_val=NB) for x_ in regs]
                for k in range(K):
                    h, i = k // (K // HALVES), k % (K // HALVES)
                    if k == 0:
                        leave(k)
                    if between is not None:
                        between(k)
                    if at is not None:
                        v.wait_ge(s.sum, HALVES * g + h + 1)
                    if k:
                        leave(k)
                    if at is not None:
                        wait(v, s.acc, K * g + k)
                        here = acc[:, bass.ds(nbs[k] * SEG, cols)]
                        v.tensor_tensor(here, here, bank[4 + HALVES * (at[1] % 2) + h][:, i * SEG:i * SEG + cols],
                                        ALU.add).then_inc(s.acc, 1)

            def sum_inverse(s, layer, t, nb, i):
                seg = acc[:, span(nb * SEG + D, 1)]
                if i == 0:
                    wait(v, s.inv, t)
                    if layer == 0:
                        v.tensor_scalar(seg_w[:, :], seg, 1e-9, 2.0, ALU.add, ALU.mult).then_inc(s.seg, 1)
                    else:
                        v.tensor_scalar(seg_w[:, :], seg, 1.0, None, ALU.max).then_inc(s.seg, 1)
                if i == 1:
                    v.wait_ge(s.seg, t + 1)
                    wait(v, s.emb, t)
                    v.reciprocal(seg_inv[:, :], seg_w[:, :]).then_inc(s.inv, 1)

            def residual(s, layer, t):
                v.wait_ge(s.lin, t + 1)
                v.wait_ge(s.xres, 16 * (t + 1))
                wait(v, s.res, t)
                if layer == 0:
                    v.scalar_tensor_tensor(out=y[:, :], in0=bank[4][:, LIN_AT:LIN_AT + D], scalar=0.0, in1=x_res[:, :],
                                           op0=ALU.max, op1=ALU.add).then_inc(s.y, 1)
                else:
                    v.tensor_tensor(y[:, :], bank[4][:, LIN_AT:LIN_AT + D], x_res[:, :], ALU.add).then_inc(s.y, 1)

            def statistics(s, t):
                v.wait_ge(s.y, t + 1)
                wait(v, s.mv, t)
                v.bn_stats(stats[:, :], y[:, :]).then_inc(s.st, 1)

            def aggregate(s, t):
                v.wait_ge(s.st, t + 1)
                wait(v, s.shift, t)
                v.sem_inc(s.go, 1)
                v.bn_aggr(mv[:, :], stats[:, :]).then_inc(s.mv, 1)

            ROOT_STEPS = 9
            ROOT_FACTOR = [1.0]
            for _ in range(3):
                ROOT_FACTOR.append(-2.0 * ROOT_FACTOR[-1] ** 3)

            def root_step(s, t, i):
                v.wait_ge(s.root, t * ROOT_STEPS + i) if i else v.wait_ge(s.mv, t + 1)
                if i == 0:
                    wait(v, s.root, t * ROOT_STEPS)
                    ins = v.tensor_scalar(var_eps[:, :], mv[:, 1:2], EPS, None, ALU.add)
                elif i == 1:
                    ins = v.tensor_scalar(half_bits[:, :], var_eps[:, :].bitcast(I32), 1, None, ALU.arith_shift_right)
                elif i == 2:
                    wait(v, s.shift, t)
                    ins = v.tensor_scalar(root[:, :].bitcast(I32), half_bits[:, :], -1.0, float(0x5F3759DF), ALU.mult, ALU.add)
                elif i % 2:
                    ins = v.scalar_tensor_tensor(out=root_sq[:, :], in0=root[:, :], scalar=var_eps[:, :], in1=root[:, :],
                                                 op0=ALU.mult, op1=ALU.mult)
                else:
                    ins = v.scalar_tensor_tensor(out=root[:, :], in0=root_sq[:, :], scalar=-3.0 * ROOT_FACTOR[i // 2 - 2] ** 2,
                                                 in1=root[:, :], op0=ALU.add, op1=ALU.mult)
                ins.then_inc(s.root, 1)

            def mean_shift(s, t):
                v.wait_ge(s.root, (t + 1) * ROOT_STEPS)
                wait(v, s.res, t)
                f = 1.0 / ROOT_FACTOR[-1]
                v.tensor_scalar(rstd[:, :], root[:, :], f, None, ALU.mult)
                v.scalar_tensor_tensor(out=shift[:, :], in0=mv[:, 0:1], scalar=-f, in1=root[:, :],
                                       op0=ALU.mult, op1=ALU.mult).then_inc(s.shift, 1)

            turn_nb = [None]

            def turn_begin(s, es, layer, r, j):
                t = turn(r, 1)
                if t is not None and j == 0:
                    turn_nb[0] = turn_is(v, turn_regs, turn_block[layer], t)

            def turn_step(s, es, layer, r, j, k):
                t = turn(r, 2)
                if t is not None and (j, k) == (0, 1):
                    residual(s, layer, t)
                if t is not None and (j, k) == (0, 3):
                    statistics(s, t)
                if t is not None and (j, k) == (1, 0):
                    aggregate(s, t)
                if t is not None and 0 <= j * K + k - K - 1 < ROOT_STEPS:
                    root_step(s, t, j * K + k - K - 1)
                if t is not None and (j, k) == (3, 2):
                    mean_shift(s, t)
                t = turn(r, 1)
                if t is not None and j == 0 and k in (1, 2):
                    if k == 1:
                        added = r * ROUND * K - (4, 2)[layer] * K
                        wait(v, es.acc, min(added, NPAIR) if isinstance(r, int) else added)
                    sum_inverse(s, layer, t, turn_nb[0], k - 1)
                if t is not None and (j, k) == (2, 0):
                    v.wait_ge(s.emb, t + 1)

            def again(s, layer):
                def body(t, nb):
                    for i in range(2):
                        sum_inverse(s, layer, t, nb, i)
                    residual(s, layer, t)
                    statistics(s, t)
                    aggregate(s, t)
                    for i in range(ROOT_STEPS):
                        root_step(s, t, i)
                    mean_shift(s, t)
                return body

            def edge0_step(r, j):
                one_hots(edge0, r, j, lambda k: hot_e[:, j, k, :], ROUND)
                at = back(r, j, 2, NG)
                if at is not None:
                    rr, jj, g = at
                    v.wait_ge(edge0.a, g + 1)
                    v.wait_ge(edge0.got[jj], slot_use(rr))
                    wait(v, edge0.logit, g - 1)
                    v.tensor_tensor(hidden[:, jj % 2, :, :],
                                    bank[2 + jj % 2][:, :].rearrange("p (k d) -> p k d", d=D),
                                    got[:, jj, :, 0:D], ALU.add).then_inc(edge0.hid, 1)
                    wait(v, edge0.weight, g - 1)

                def logits(k):
                    if at is not None:
                        if k == 0:
                            v.wait_ge(edge0.hid, at[2] + 1)
                        h = hidden[:, at[1] % 2, k, :]
                        ins = v.scalar_tensor_tensor(out=h, in0=h, scalar=0.0, in1=w2[:, :], op0=ALU.max, op1=ALU.mult,
                                                     accum_out=logit[:, at[1] % 2, k:k + 1])
                        if k == K - 1:
                            ins.then_inc(edge0.logit, 1)

                turn_begin(node0, edge0, 0, r, j)
                add_sums(edge0, r, j, 4, SEG, logits, lambda k: turn_step(node0, edge0, 0, r, j, k))

            def edge1_step(r, j):
                one_hots(edge1, r, j, lambda k: whot[:, j % 2, k, :], 2)
                turn_begin(node1, edge1, 1, r, j)
                add_sums(edge1, r, j, 2, D + 1, None, lambda k: turn_step(node1, edge1, 1, r, j, k))

            places(sort0, 0, True)
            v.wait_ge(s_cnt1, NB)
            count(1, NB).then_inc(s_bel, 1)
            pairs(pair0, 0)
            for c in range(NCH):
                rows_float(pair0, 0, c)
            turns(0)
            v.wait_ge(s_st, 3)
            link(v.tensor_copy(start[1][:, 0:NBX], bank[3][:, 0:NBX]))
            v.wait_ge(s_bel, 2)
            v.wait_ge(s_list1, 32)
            link(v.memset(acc[:, :], 0.0))
            v.wait_ge(pair0.bld, 16)
            v.wait_ge(pair0.done, 2 * NCH)
            run_steps(v, NG, EDGE_LAG, edge0_step)

            flag = v.value_load(unsorted_i[0:1, 0:1], min_val=0, max_val=1)
            with v.If(flag):
                for j in range(ROUND):
                    v.wait_ge(sort0.wrote[j], slot_use(ROUNDS_SORT - 1))
                v.wait_ge(sort0.base, NQ + 1)
                v.tensor_copy(base[:, :], start[1][:, 0:NBX]).then_inc(sort1.base, 1)
                places(sort1, 1, False)
            v.wait_ge(edge0.acc, NPAIR)
            pairs(pair1, 1)
            for c in range(NCH - TAIL_STEPS):
                rows_float(pair1, 1, c)
            for r in TURN_TAIL:
                for j in range(ROUND):
                    c = (r - TURN_TAIL[0]) * ROUND + j + NCH - TAIL_STEPS
                    if 0 <= c < NCH:
                        rows_float(pair1, 1, c)
                    turn_begin(node0, edge0, 0, r, j)
                    for k in range(K):
                        turn_step(node0, edge0, 0, r, j, k)
            turns(1)
            all_blocks_again(v, 0, again(node0, 0))
            v.wait_ge(node0.res, NTICK)
            link(v.memset(acc[:, :], 0.0))
            v.wait_ge(pair1.done, 2 * NCH)
            v.wait_ge(pair1.bld, 16)
            run_steps(v, NG, EDGE_LAG, edge1_step)
            v.wait_ge(edge1.acc, NPAIR)
            for r in TURN_TAIL:
                for j in range(ROUND):
                    turn_begin(node1, edge1, 1, r, j)
                    for k in range(K):
                        turn_step(node1, edge1, 1, r, j, k)
            all_blocks_again(v, 1, again(node1, 1))


_INS = ["x", "src", "dst", "L0_gnn_W1", "L0_gnn_b1", "L0_gnn_W2", "L0_gnn_b2", "L0_gnn_Wl", "L0_gnn_bl", "L1_gnn_W", "L1_gnn_b"]


def kernel(**inputs):
    import numpy as _np
    import concourse.bacc as _bacc
    from concourse import mybir as _mybir
    from concourse.bass_utils import run_bass_kernel_spmd as _run

    nc = _bacc.Bacc("TRN2", target_bir_lowering=False, num_devices=1)
    arrays, args = {}, []
    for name in _INS:
        a = _np.ascontiguousarray(inputs[name])
        arrays[f"in_{name}_dram"] = a
        args.append(nc.dram_tensor(f"in_{name}_dram", a.shape, _mybir.dt.from_np(a.dtype), kind="ExternalInput").ap())
    out = nc.dram_tensor("out_0_dram", (N, D), _mybir.dt.float32, kind="ExternalOutput").ap()
    build(nc, *args, out)
    r = _run(nc, [arrays], core_ids=[0])
    return r.results[0]["out_0_dram"]
```

```python
from contextlib import ExitStack

import concourse.bass as bass
from concourse import mybir

F32 = mybir.dt.float32
BF16 = mybir.dt.bfloat16
I32 = mybir.dt.int32
ALU = mybir.AluOpType
ACT = mybir.ActivationFunctionType
AX_X = mybir.AxisListType.X

P = 128
N = 12500
D = 128
E = 200000
NB = -(-N // P)
NBX = NB + 1
ROWS = NBX * P
TAIL = N - (NB - 1) * P
PAD_KEY = NB * P

CW = E // P
REST = E - CW * P
ROUND = 4
K = 4
NQ = ROUND * -(-(CW + 1) // (K * ROUND))
NT = NQ * K
ROUNDS_SORT = NQ // ROUND
LOW = 8
HIGH = -(-NBX // LOW)
GT = 16
NGT = NT // GT
REAL_ROWS = CW + 1
NCH = -(-(REAL_ROWS + NB - 1) // P)
NPAIR = NCH * P
NG = NPAIR // K
TURNS = NG // ROUND + 2
HALVES = 2
SEG = D + 2
LIN_AT = K // 2 * SEG
GW = 2 * D + 1
EPS = 1e-5
assert ROUNDS_SORT == NB and NG % ROUND == 0 and TURNS <= P
assert LOW * GT <= P and NGT % 14 == 0


def run_steps(eng, n, lag, step, per=ROUND, head=2):
    rounds = n // per
    for s in range(head * per):
        step(s // per, s % per)
    with eng.Fori(head, rounds) as r:
        for j in range(per):
            step(r, j)
    for s in range(rounds * per, n + lag):
        step(s // per, s % per)


def back(r, j, lag, n, per=ROUND):
    r, j = r + (j - lag) // per, (j - lag) % per
    if isinstance(r, int) and not 0 <= r * per + j < n:
        return None
    return r, j, r * per + j


def span(start, size):
    return slice(start, start + size) if isinstance(start, int) else bass.ds(start, size)


def wait(eng, sem, value):
    if not isinstance(value, int) or value > 0:
        eng.wait_ge(sem, value)


def build(nc, x, src, dst, W1, b1, W2, b2, Wl, bl, W, b, out):
    with ExitStack() as ctx:
        def sb(name, shape, dt):
            return ctx.enter_context(nc.sbuf_tensor(name, shape, dt))

        def sem(name):
            return ctx.enter_context(nc.semaphore(name))

        def dram(name, shape, dt):
            return nc.dram_tensor(name, shape, dt).ap()

        table0 = dram("table0", (ROWS, 2 * D), F32)
        table1 = dram("table1", (ROWS, D), F32)
        lists = [dram(f"list{n}", (NT, 2 * P), I32) for n in range(2)]
        blocks_dram = [dram(f"blocks{n}", (NCH, P), I32) for n in range(2)]

        ident = sb("ident", [P, P], F32)
        ident_b = sb("ident_b", [P, P], BF16)
        ones = sb("ones", [P, P], F32)
        ones_b = sb("ones_b", [P, P], BF16)
        upper_b = sb("upper_b", [P, P], BF16)
        zeros = sb("zeros", [P, 2 * D], F32)
        iota_b = sb("iota_b", [P, P], BF16)
        iota_f = sb("iota_f", [P, P], F32)
        bound_f = sb("bound_f", [P, NBX], F32)
        digit_i = sb("digit_i", [P, 3], I32)
        digit_f = sb("digit_f", [P, 2], F32)
        same_low = sb("same_low", [P, LOW], F32)
        same_tile = sb("same_tile", [P, GT], F32)
        pair_no = sb("pair_no", [P, NCH], F32)
        turn_no = sb("turn_no", [P, 2], F32)
        w1 = sb("w1", [P, 2, D], F32)
        w2 = sb("w2", [P, D], F32)
        wl = sb("wl", [P, D], F32)
        w_in = sb("w_in", [P, D], F32)
        wt = sb("wt", [P, D], F32)
        b1_bc = sb("b1_bc", [P, D], F32)
        b2_bc = sb("b2_bc", [P, 1], F32)
        bl_bc = sb("bl_bc", [P, D], F32)
        b_bc = sb("b_bc", [P, D], F32)

        edge = [sb("edge_src", [P, NT], I32), sb("edge_dst", [P, NT], I32)]
        shift_tail = sb("shift_tail", [1, 2, REST], I32)
        hi = [sb("hi_src", [P, NT], BF16), sb("hi_dst", [P, NT], BF16)]
        below = sb("below_dst", [P, NBX], F32)
        hist_prod = sb("hist_prod", [LOW * GT, HIGH, GT], F32)
        hist_high = sb("hist_high", [LOW * GT, HIGH], F32)
        hist_all = sb("hist_all", [LOW * GT, HIGH, LOW], F32)
        start = [sb("start_src", [P, NBX + 1], F32), sb("start_dst", [P, NBX + 1], F32)]
        unsorted = sb("unsorted", [P, 2], F32)
        unsorted_i = sb("unsorted_i", [1, 1], I32)
        base = sb("base", [P, NBX], F32)
        hot = sb("hot", [P, 2, K, NBX], BF16)
        rank_prod = sb("rank_prod", [P, K, NBX], F32)
        pos = sb("pos", [P, ROUND, K], I32)
        rec = sb("rec", [P, ROUND, K, 2], I32)

        start_i = sb("start_i", [P, NBX + 1], I32)
        first_i = sb("first_i", [P, NBX + 1], I32)
        first_f = sb("first_f", [P, NBX + 1], F32)
        last_i = sb("last_i", [P, NBX], I32)
        last_f = sb("last_f", [P, NBX], F32)
        npair = sb("npair", [P, NB], F32)
        pair_end = sb("pair_end", [P, NB], F32)
        shift_f = sb("shift_f", [P, NBX], F32)
        pick = sb("pick", [P, NBX], F32)
        pair_block = sb("pair_block", [P, NCH], F32)
        pair_block_i = [sb(f"pair_block_i{n}", [P, NCH], I32) for n in range(2)]
        pair_lo = [sb(f"pair_lo{n}", [P, NCH], F32) for n in range(2)]
        pair_row = sb("pair_row", [P, NCH], F32)
        pair_row_i = [sb(f"pair_row_i{n}", [P, NCH], I32) for n in range(2)]
        blocks = sb("blocks", [1, NPAIR], I32)
        list_row = sb("list_row", [P, 2, P, 2], I32)
        list_f = sb("list_f", [P, 2, P], F32)
        local = sb("local", [P, NPAIR], F32)
        other = sb("other", [P, NPAIR], I32)

        a_tab = sb("a_tab", [P, NBX * D], F32)
        acc = sb("acc", [P, NBX * SEG], F32)
        acc_col = acc[:, :].rearrange("p (n s) -> p n s", s=SEG)
        keyf = acc[:, 0:NT]
        unused = acc[:, NT:2 * NT]
        stage = acc[:, 4 * NT:6 * NT].bitcast(I32).rearrange("p (c f) -> p c f", f=2)
        shifted = acc[:, 6 * NT:6 * NT + CW].bitcast(I32)
        digits_at = 6 * NT + CW
        digit = [acc[:, digits_at + n * NT // 2:digits_at + (n + 1) * NT // 2].bitcast(BF16) for n in range(2)]
        digit_raw = [local[:, 0:NT].bitcast(I32), acc[:, 4 * NT:5 * NT].bitcast(I32)]
        hot_high = a_tab[:, 0:HIGH * NT // 2].bitcast(BF16).rearrange("p (d t) -> p d t", t=NT)
        hot_low = acc[:, 0:LOW * NT // 2].bitcast(BF16).rearrange("p (g d t) -> p g d t", d=LOW, t=GT)
        hot_low_flat = acc[:, 0:LOW * NT // 2].bitcast(BF16)
        xb = sb("xb", [P, D], F32)
        x_res = sb("x_res", [P, D], F32)
        xbT = sb("xbT", [P, D], F32)
        bx = sb("bx", [P, D], F32)
        idx = sb("idx", [P, ROUND, K], I32)
        got = sb("got", [P, ROUND, K, GW], F32)
        hot_e = sb("hot_e", [P, ROUND, K, P], BF16)
        hot_n = sb("hot_n", [P, 2, K, P], F32)
        hidden = sb("hidden", [P, 2, K, D], F32)
        logit = sb("logit", [P, 2, K], F32)
        weight = sb("weight", [P, 2, K], F32)
        whot = sb("whot", [P, 2, K, P], F32)
        done_by = sb("done_by", [P, 2], F32)
        turn_f = sb("turn_f", [1, TURNS - 1], F32)
        turn_skip = sb("turn_skip", [1, TURNS - 1], F32)
        turn_block = [sb(f"turn_block{n}", [1, TURNS - 1], I32) for n in range(2)]
        turn_store = [sb(f"turn_store{n}", [1, TURNS - 1], I32) for n in range(2)]
        late = sb("late", [1, 2], I32)
        seg_w = sb("seg_w", [P, 1], F32)
        seg_inv = sb("seg_inv", [P, 1], F32)
        has_edge = sb("has_edge", [P, 1], F32)
        keep_x = sb("keep_x", [P, 1], F32)
        scale = sb("scale", [P, 1], F32)
        emb_x = sb("emb_x", [P, D], F32)
        emb_e = sb("emb_e", [P, D], F32)
        embT = sb("embT", [P, D], F32)
        y = sb("y", [P, D], F32)
        result = sb("result", [P, D], F32)
        stats = sb("stats", [P, 6], F32)
        mv = sb("mv", [P, 2], F32)
        var_eps = sb("var_eps", [P, 1], F32)
        half_bits = sb("half_bits", [P, 1], I32)
        root = sb("root", [P, 1], F32)
        root_sq = sb("root_sq", [P, 1], F32)
        rstd = sb("rstd", [P, 1], F32)
        shift = sb("shift", [P, 1], F32)

        bank = [ctx.enter_context(nc.psum_tensor(f"bank{n}", [P, 512], F32)) for n in range(8)]
        bank_b = [t[:, 0:K * P // 2].bitcast(BF16) for t in bank]

        s_c = sem("constants")
        s_cv = sem("constants_vector")
        s_w = sem("weights_loaded")
        s_wt = sem("w_turned")
        s_wtc = sem("w_turned_copied")
        s_e = [sem("src_loaded"), sem("dst_loaded")]
        s_pad = sem("edge_padding")
        s_tab = sem("tables_filled")
        s_chain = sem("vector_chain")
        s_key = sem("keys_ready")
        s_digit = sem("digits_ready")
        s_planes = sem("digit_one_hots_ready")
        s_joint = sem("joint_counts_ready")
        s_joint_row = sem("joint_counts_spread")
        s_bel = sem("below_counts")
        s_st = sem("starts_summed")
        s_flag = sem("flag_ready")
        s_copy1 = sem("list1_written")
        s_list1 = sem("list1_ready")
        s_cnt1 = sem("dst_counted")
        s_done_by = sem("complete_blocks_counted")
        s_done_row = sem("complete_blocks_as_row")
        s_turns = sem("turns_ready")
        s_flag0 = sem("descents_counted")
        s_idb = sem("ident_bf16_ready")

        class SortSems:
            def __init__(self, tag):
                self.hot = sem(f"{tag}_hot_ready")
                self.rank = sem(f"{tag}_rank_ready")
                self.base = sem(f"{tag}_base_ready")
                self.prod = sem(f"{tag}_prod_ready")
                self.pos = sem(f"{tag}_pos_ready")
                self.rec = sem(f"{tag}_records_ready")
                self.go = sem(f"{tag}_scatter_go")
                self.wrote = [sem(f"{tag}_scattered{n}") for n in range(ROUND)]

        sort0, sort1 = SortSems("sort0"), SortSems("sort1")

        s_xld = sem("x_block_loaded")
        s_xT = sem("x_turned")
        s_xTc = sem("x_turned_copied")
        s_ab = sem("ab_ready")
        s_aw = sem("a_written")
        s_bw = sem("b_written")
        s_bst = sem("b_stored")

        class PairSems:
            def __init__(self, tag):
                self.calc = sem(f"{tag}_pairs_ready")
                self.bst = sem(f"{tag}_blocks_stored")
                self.bld = sem(f"{tag}_blocks_loaded")
                self.got = [sem(f"{tag}_rows_gathered{n}") for n in range(2)]
                self.flt = sem(f"{tag}_rows_float")
                self.turn = sem(f"{tag}_rows_turned")
                self.done = sem(f"{tag}_columns_ready")

        pair0, pair1 = PairSems("pair0"), PairSems("pair1")

        class EdgeSems:
            def __init__(self, tag, attends):
                self.idx = sem(f"{tag}_idx_ready")
                self.go = sem(f"{tag}_gather_go")
                self.got = [sem(f"{tag}_gathered{n}") for n in range(ROUND)]
                self.hot = sem(f"{tag}_hot_ready")
                if attends:
                    self.turn = sem(f"{tag}_hot_turned")
                    self.turnc = sem(f"{tag}_hot_turned_copied")
                    self.a = sem(f"{tag}_a_spread")
                    self.hid = sem(f"{tag}_hidden_ready")
                    self.logit = sem(f"{tag}_logit_ready")
                    self.weight = sem(f"{tag}_weight_ready")
                    self.whot = sem(f"{tag}_weighted_hot_ready")
                self.sum = sem(f"{tag}_pair_summed")
                self.acc = sem(f"{tag}_pair_added")

        edge0, edge1 = EdgeSems("edge0", True), EdgeSems("edge1", False)

        class NodeSems:
            def __init__(self, tag):
                self.x = sem(f"{tag}_x_loaded")
                self.xres = sem(f"{tag}_residual_loaded")
                self.seg = sem(f"{tag}_sum_read")
                self.inv = sem(f"{tag}_sum_inverse_ready")
                self.fac = sem(f"{tag}_factors_ready")
                self.emb = sem(f"{tag}_emb_ready")
                self.turn = sem(f"{tag}_emb_turned")
                self.turnc = sem(f"{tag}_emb_turned_copied")
                self.lin = sem(f"{tag}_linear_ready")
                self.y = sem(f"{tag}_y_ready")
                self.st = sem(f"{tag}_stats_ready")
                self.go = sem(f"{tag}_aggregate_go")
                self.mv = sem(f"{tag}_meanvar_ready")
                self.root = sem(f"{tag}_root_steps")
                self.shift = sem(f"{tag}_shift_ready")
                self.res = sem(f"{tag}_result_ready")
                self.out = sem(f"{tag}_result_stored")

        node0, node1 = NodeSems("node0"), NodeSems("node1")

        def slot_use(r):
            return (r + 1) * 16 * K

        def block_rows(table, nb, cols=None):
            view = table.rearrange("(n p) d -> n p d", p=P)
            return view[nb] if cols is None else view[nb, :, cols]

        SORT_LAG = 1
        EDGE_LAG = ROUND
        TURN_TAIL = range((NG + EDGE_LAG) // ROUND, TURNS + 2)
        TAIL_STEPS = len(TURN_TAIL) * ROUND

        def turn(r, lag):
            t = r - lag
            return None if isinstance(t, int) and not 0 <= t < TURNS else t

        def turn_is(eng, regs, table, t):
            if isinstance(t, int) and t == TURNS - 1:
                return NB - 1
            eng.load(regs, table[0:1, span(t, 1)])
            return eng.snap(regs[0], min_val=0, max_val=NB if any(table is t_ for t_ in turn_block) else NB - 2)

        def wait_again(eng, layer, s):
            flag_late = eng.value_load(late[0:1, layer:layer + 1], min_val=0, max_val=1)
            with eng.If(flag_late):
                eng.wait_ge(s.out, 16 * (TURNS + NB - 1))

        def all_blocks_again(eng, layer, body):
            flag_late = eng.value_load(late[0:1, layer:layer + 1], min_val=0, max_val=1)
            with eng.If(flag_late):
                with eng.Fori(0, NB - 1) as nb:
                    body(nb + TURNS, nb)

        block = ctx.enter_context(nc.Block())

        @block.sync
        def _(sp):
            flat = [v.rearrange("(p c) -> p c", c=CW) for v in (src[0:P * CW], dst[0:P * CW])]
            sp.wait_ge(s_pad, 2)
            for n, v in enumerate((src, dst)):
                sp.dma_start(edge[n][:, 0:CW], flat[n]).then_inc(s_e[n], 16)
                sp.dma_start(edge[n][0:REST, CW:CW + 1],
                             v[P * CW:E].rearrange("(p c) -> p c", c=1)).then_inc(s_e[n], 16)
            sp.dma_start(shifted[:, :], dst[1:P * CW + 1].rearrange("(p c) -> p c", c=CW)).then_inc(s_e[1], 16)
            sp.dma_start(shift_tail[:, 0, 0:REST - 1], dst[P * CW:E - 1].rearrange("(a c) -> a c", a=1)).then_inc(s_e[1], 16)
            sp.dma_start(shift_tail[:, 1, 0:REST - 1], dst[P * CW + 1:E].rearrange("(a c) -> a c", a=1)).then_inc(s_e[1], 16)
            sp.dma_start(table0[0:N, D:2 * D], x).then_inc(s_tab, 16)
            sp.wait_ge(s_cv, 1)
            pad = ROWS - N
            sp.dma_start(table0[N:N + P, D:2 * D], zeros[:, 0:D]).then_inc(s_tab, 16)
            sp.dma_start(table0[N + P:ROWS, D:2 * D], zeros[0:pad - P, 0:D]).then_inc(s_tab, 16)
            sp.dma_start(block_rows(table0, NB, slice(0, D)), zeros[:, 0:D]).then_inc(s_tab, 16)
            sp.dma_start(block_rows(table1, NB), zeros[:, 0:D]).then_inc(s_tab, 16)
            sp.dma_start(w1[:, :, :], W1.rearrange("(t p) d -> p t d", p=P)).then_inc(s_w, 16)
            sp.dma_start(w2[:, :], W2.rearrange("d a -> a d").to_broadcast([P, D])).then_inc(s_w, 16)
            sp.dma_start(wl[:, :], Wl).then_inc(s_w, 16)
            sp.dma_start(w_in[:, :], W).then_inc(s_w, 16)
            for tile, v in ((b1_bc, b1), (bl_bc, bl), (b_bc, b), (b2_bc, b2)):
                sp.dma_start(tile[:, :], v.rearrange("(a d) -> a d", a=1).to_broadcast([P, v.shape[0]])).then_inc(s_w, 16)

            sp.wait_ge(s_copy1, 2)
            view = lists[1].rearrange("t (p c) -> (t p) c", c=2)
            sp.dma_start(view[0:P * CW, :].rearrange("(p c) f -> p (c f)", c=CW),
                         stage[:, 0:CW, :].rearrange("p c f -> p (c f)")).then_inc(s_list1, 16)
            sp.dma_start(view[P * CW:P * (CW + 1), :], stage[:, CW, :]).then_inc(s_list1, 16)

            sp.wait_ge(s_tab, 80)
            sp.dma_start(xb[:, :], block_rows(table0, 0, slice(D, 2 * D))).then_inc(s_xld, 16)
            with sp.Fori(1, NB) as nb:
                sp.wait_ge(s_xT, nb)
                sp.dma_start(xb[:, :], block_rows(table0, nb, slice(D, 2 * D))).then_inc(s_xld, 16)
                sp.wait_ge(s_bw, nb)
                sp.dma_start(block_rows(table0, nb - 1, slice(0, D)), bx[:, :]).then_inc(s_bst, 16)
            sp.wait_ge(s_bw, NB)
            sp.dma_start(block_rows(table0, NB - 1, slice(0, D)), bx[:, :]).then_inc(s_bst, 16)

            def pair_blocks(s, n):
                sp.wait_ge(s.calc, 1)
                with nc.allow_non_contiguous_dma(reason="13 columns of block numbers"):
                    sp.dma_start(blocks_dram[n].rearrange("c p -> p c"), pair_block_i[n][:, :]).then_inc(s.bst, 16)
                sp.wait_ge(s.bst, 16)
                sp.dma_start(blocks[:, :], blocks_dram[n].rearrange("(a c) p -> a (c p)", a=1)).then_inc(s.bld, 16)

            regs = [sp.alloc_register("sp_block")]

            def load_x(s, table, cols, t, nb):
                wait(sp, s.emb, t)
                sp.dma_start(xb[:, :], block_rows(table, nb, cols)).then_inc(s.x, 16)

            def load_residual(s, table, cols, t, nb):
                wait(sp, s.y, t)
                sp.dma_start(x_res[:, :], block_rows(table, nb, cols)).then_inc(s.xres, 16)

            def store(s, target, last_rows, t, nb):
                sp.wait_ge(s.res, t + 1)
                if isinstance(nb, int) and nb == NB - 1:
                    sp.dma_start(target[nb * P:nb * P + last_rows, :], result[0:last_rows, :]).then_inc(s.out, 16)
                else:
                    view = target[0:(NB - 1) * P, :].rearrange("(n p) d -> n p d", p=P)
                    sp.dma_start(view[nb], result[:, :]).then_inc(s.out, 16)

            def node_io(s, layer, table, cols, target, last_rows):
                def step(r, j):
                    t = turn(r, 1)
                    if t is not None:
                        load_residual(s, table, cols, t, turn_is(sp, regs, turn_block[layer], t))
                    t = turn(r, 0)
                    if t is not None and layer == 0:
                        load_x(s, table, cols, t, turn_is(sp, regs, turn_block[layer], t))
                    t = turn(r, 2)
                    if t is not None:
                        store(s, target, last_rows, t, turn_is(sp, regs, turn_store[layer], t))

                def again(t, nb):
                    if layer == 0:
                        load_x(s, table, cols, t, nb)
                    load_residual(s, table, cols, t, nb)
                    store(s, target, last_rows, t, nb)

                run_steps(sp, NG // ROUND, EDGE_LAG // ROUND, step, 1)
                if layer == 0:
                    sp.wait_ge(edge0.a, NG)
                    sp.wait_ge(edge0.acc, NPAIR)
                    pair_blocks(pair1, 1)
                for r in TURN_TAIL:
                    step(r, 0)
                sp.wait_ge(s.out, 16 * TURNS)
                all_blocks_again(sp, layer, again)

            pair_blocks(pair0, 0)
            sp.wait_ge(s_xT, NB)
            sp.wait_ge(s_turns, 1)
            node_io(node0, 0, table0, slice(D, 2 * D), table1, P)
            sp.wait_ge(node0.out, 16 * TURNS)
            wait_again(sp, 0, node0)
            sp.wait_ge(s_turns, 2)
            node_io(node1, 1, table1, slice(0, D), out, TAIL)
            wait_again(sp, 1, node1)

        @block.gpsimd
        def _(pool):
            def ramp(tile, step, n, partition, base=0):
                pool.iota(tile[:, :], [[step, n]], base=base, channel_multiplier=partition,
                          allow_small_or_imprecise_dtypes=True).then_inc(s_c, 1)

            ramp(bound_f, P, NBX, 0)
            ramp(iota_f, 1, P, 0)
            ramp(iota_b, 1, P, 0)
            ramp(pair_no, P, NCH, 1)
            ramp(turn_no, 2 * K, 2, ROUND * K)
            pool.wait_ge(s_cv, 3)
            pool.affine_select(out=ident[:, :], in_=zeros[:, 0:P], compare_op=ALU.not_equal, fill=1.0, base=0,
                               pattern=[[-1, P]], channel_multiplier=1).then_inc(s_c, 1)
            pool.affine_select(out=upper_b[:, :], in_=ones_b[:, :], compare_op=ALU.is_gt, fill=0.0, base=0,
                               pattern=[[1, P]], channel_multiplier=-1).then_inc(s_c, 1)

            def scatter(s, n):
                target = lists[n].rearrange("t (p c) -> (t p) c", c=2)
                def step(r, j):
                    q = r * ROUND + j
                    pool.wait_ge(s.pos, q + 1)
                    pool.wait_ge(s.rec, q + 1)
                    pool.sem_inc(s.go, 1)
                    for k in range(K):
                        pool.indirect_dma_start(target, bass.IndirectOffsetOnAxis(pos[:, j, k:k + 1], 0),
                                                rec[:, j, k, :], None).then_inc(s.wrote[j], 16)
                run_steps(pool, NQ, 0, step)
                for j in range(ROUND):
                    pool.wait_ge(s.wrote[j], slot_use(ROUNDS_SORT - 1))

            def gather_rows(s, n):
                pool.wait_ge(s.calc, 1)
                for c in range(NCH):
                    if c >= 2:
                        pool.wait_ge(s.flt, 2 * (c - 1))
                    pool.indirect_dma_start(list_row[:, c % 2, :, :].rearrange("p e f -> p (e f)"), None, lists[n],
                                            bass.IndirectOffsetOnAxis(pair_row_i[n][:, c:c + 1], 0)).then_inc(s.got[c % 2], 16)

            def gather_edges(s, table, width):
                def step(r, j):
                    pool.wait_ge(s.idx, r * ROUND + j + 1)
                    pool.sem_inc(s.go, 1)
                    for k in range(K):
                        off = 2 * D - width
                        pool.indirect_dma_start(got[:, j, k, off:off + width], None, table,
                                                bass.IndirectOffsetOnAxis(idx[:, j, k:k + 1], 0)).then_inc(s.got[j], 16)
                run_steps(pool, NG, 0, step)

            scatter(sort0, 0)
            gather_rows(pair0, 0)
            pool.wait_ge(s_bst, 16 * NB)
            gather_edges(edge0, table0, 2 * D)
            pool.wait_ge(s_flag, 1)
            pool.wait_ge(s_list1, 32)
            flag = pool.value_load(unsorted_i[0:1, 0:1], min_val=0, max_val=1)
            with pool.If(flag):
                scatter(sort1, 1)
            pool.wait_ge(pair0.flt, 2 * NCH)
            gather_rows(pair1, 1)
            pool.wait_ge(node0.out, 16 * TURNS)
            wait_again(pool, 0, node0)
            gather_edges(edge1, table1, D)

        @block.scalar
        def _(act):
            for n in range(2):
                act.wait_ge(s_digit, n + 1)
                act.copy(digit[n], digit_raw[n]).then_inc(s_key, 1)

            def sort_side(s, with_blocks):
                def step(r, j):
                    q = r * ROUND + j
                    if not (isinstance(r, int) and r < 1):
                        act.wait_ge(s.wrote[j], slot_use(r - 1))
                    for f in range(2):
                        act.copy(rec[:, j, :, f], edge[f][:, span(q * K, K)]).then_inc(s.rec, 1)
                    act.wait_ge(s.rank, q + 1)
                    act.wait_ge(s.base, q + 1)
                    act.copy(base[:, :], bank[j % 2][:, K * NBX:(K + 1) * NBX]).then_inc(s.base, 1)
                    if with_blocks and j == 0:
                        act.wait_ge(s_xT, r + 1)
                        wait(act, s_ab, r)
                        act.copy(xbT[:, :], bank[2][:, 0:P]).then_inc(s_xTc, 1)
                    if with_blocks and j == 2:
                        act.wait_ge(s_ab, r + 1)
                        wait(act, s_bst, 16 * r)
                        act.copy(bx[:, :], bank[4][:, 0:D]).then_inc(s_bw, 1)
                run_steps(act, NQ, 0, step)

            def pair_columns(s, c):
                act.wait_ge(s.turn, c + 1)
                act.copy(local[:, c * P:(c + 1) * P], bank[6][:, 0:P]).then_inc(s.done, 1)
                act.copy(other[:, c * P:(c + 1) * P], bank[6][:, P:2 * P]).then_inc(s.done, 1)

            def indices(s, r, j):
                at = back(r, j, 0, NG)
                if at is not None:
                    g = at[2]
                    wait(act, s.sum, HALVES * (g - ROUND + 1))
                    act.copy(idx[:, j, :], other[:, span(g * K, K)]).then_inc(s.idx, 1)

            def copy_turned(s, t):
                act.wait_ge(s.turn, t + 1)
                wait(act, s.lin, t)
                act.copy(embT[:, :], bank[0][:, 2 * P:3 * P]).then_inc(s.turnc, 1)

            def embed(s, layer, t, nb):
                edges = nb * SEG + (D + 1, D)[layer]
                act.wait_ge(s.inv, t + 1)
                act.activation(has_edge[:, :], acc[:, span(edges, 1)], ACT.Sign).then_inc(s.fac, 1)
                act.wait_ge(s.fac, t * (3 - layer) + 1)
                act.activation(scale[:, :], seg_inv[:, :], ACT.Copy, scale=has_edge[:, :]).then_inc(s.fac, 1)
                if layer == 0:
                    act.activation(keep_x[:, :], has_edge[:, :], ACT.Copy, scale=-0.5, bias=1.0).then_inc(s.fac, 1)
                wait(act, s.turn, t)
                act.wait_ge(s.fac, t * (3 - layer) + 3 - layer)
                if layer == 0:
                    act.activation(emb_e[:, :], acc[:, span(nb * SEG, D)], ACT.Copy, scale=scale[:, :])
                    act.wait_ge(s.x, 16 * (t + 1))
                    act.activation(emb_x[:, :], xb[:, :], ACT.Copy, scale=keep_x[:, :]).then_inc(s.emb, 1)
                else:
                    act.activation(emb_e[:, :], acc[:, span(nb * SEG, D)], ACT.Copy, scale=scale[:, :]).then_inc(s.emb, 1)

            def normalise(s, t):
                act.wait_ge(s.shift, t + 1)
                wait(act, s.out, 16 * t)
                act.activation(result[:, :], y[:, :], ACT.Identity, scale=rstd[:, :], bias=shift[:, :]).then_inc(s.res, 1)

            regs = [act.alloc_register("act_block")]

            def turn_step(s, layer, r, j):
                t = turn(r, 1)
                if t is not None and j == 2:
                    copy_turned(s, t)

            def turn_middle(s, layer, r, j):
                t = turn(r, 1)
                if t is not None and j == 1:
                    embed(s, layer, t, turn_is(act, regs, turn_block[layer], t))

            def turn_late(s, layer, r, j):
                t = turn(r, 2)
                if t is not None and j == 3:
                    normalise(s, t)

            def again(s, layer):
                def body(t, nb):
                    embed(s, layer, t, nb)
                    copy_turned(s, t)
                    normalise(s, t)
                return body

            def edge0_step(r, j):
                indices(edge0, r, j)
                at = back(r, j, 0, NG)
                if at is not None:
                    act.wait_ge(edge0.turn, at[2] + 1)
                turn_step(node0, 0, r, j)
                if at is not None:
                    g = at[2]
                    wait(act, edge0.a, g - 1)
                    act.copy(hot_n[:, j % 2, :, :].rearrange("p k n -> p (k n)"), bank_b[j % 2]).then_inc(edge0.turnc, 1)
                turn_middle(node0, 0, r, j)
                at = back(r, j, 2, NG)
                if at is not None:
                    _, jj, g = at
                    act.wait_ge(edge0.logit, g + 1)
                    act.activation(weight[:, jj % 2, :], logit[:, jj % 2, :], ACT.Sigmoid, bias=b2_bc[:, :]).then_inc(edge0.weight, 1)
                    act.wait_ge(edge0.weight, g + 1)
                    wait(act, edge0.sum, HALVES * (g - 1))
                    for k in range(K):
                        last = act.activation(whot[:, jj % 2, k, :], hot_e[:, jj, k, :], ACT.Copy,
                                              scale=weight[:, jj % 2, k:k + 1])
                    last.then_inc(edge0.whot, 1)
                turn_late(node0, 0, r, j)

            def edge1_step(r, j):
                indices(edge1, r, j)
                turn_step(node1, 1, r, j)
                turn_middle(node1, 1, r, j)
                turn_late(node1, 1, r, j)

            for n in range(2):
                act.wait_ge(s_e[n], (32, 80)[n])
            sort_side(sort0, True)
            for c in range(NCH):
                pair_columns(pair0, c)
            act.wait_ge(s_w, 16 * 8)
            run_steps(act, NG, EDGE_LAG, edge0_step)
            act.wait_ge(s_flag, 1)
            flag = act.value_load(unsorted_i[0:1, 0:1], min_val=0, max_val=1)
            with act.If(flag):
                for j in range(ROUND):
                    act.wait_ge(sort0.wrote[j], slot_use(ROUNDS_SORT - 1))
                sort_side(sort1, False)
            act.wait_ge(edge0.sum, HALVES * NG)
            for c in range(NCH - TAIL_STEPS):
                pair_columns(pair1, c)
            for r in TURN_TAIL:
                for j in range(ROUND):
                    c = (r - TURN_TAIL[0]) * ROUND + j + NCH - TAIL_STEPS
                    if 0 <= c < NCH:
                        pair_columns(pair1, c)
                    turn_step(node0, 0, r, j)
                    turn_middle(node0, 0, r, j)
                    turn_late(node0, 0, r, j)
            all_blocks_again(act, 0, again(node0, 0))
            run_steps(act, NG, EDGE_LAG, edge1_step)
            for r in TURN_TAIL:
                for j in range(ROUND):
                    turn_step(node1, 1, r, j)
                    turn_middle(node1, 1, r, j)
                    turn_late(node1, 1, r, j)
            all_blocks_again(act, 1, again(node1, 1))

        @block.tensor
        def _(pe):
            regs = [pe.alloc_register(f"pe_block{k}") for k in range(K)]

            pe.wait_ge(s_cv, 3)
            pe.wait_ge(s_c, 7)
            pe.wait_ge(s_idb, 1)
            def joint(g, start=False, stop=False):
                return pe.matmul(bank[0][0:LOW * GT, 0:HIGH * GT], hot_low_flat[:, span(g * (LOW * GT), LOW * GT)],
                                 hot_high[:, :, span(g * GT, GT)], start=start, stop=stop)

            for half in range(2):
                first = half * NGT // 2
                pe.wait_ge(s_planes, half + 1)
                for i in range(7):
                    joint(first + i, start=(half == 0 and i == 0))
                with pe.Fori(1, NGT // 14 - 1) as g7:
                    for i in range(7):
                        joint(g7 * 7 + (first + i))
                for g in range(first + NGT // 2 - 7, first + NGT // 2):
                    last = joint(g, stop=(g == NGT - 1))
            last.then_inc(s_joint, 1)
            pe.wait_ge(s_flag0, 1)
            pe.matmul(bank[7][:, 0:2], ones[:, :], unsorted[:, :], start=True, stop=True).then_inc(s_st, 1)
            pe.wait_ge(s_w, 16 * 8)
            pe.transpose(bank[2][:, 0:P], w_in[:, :], ident[:, :]).then_inc(s_wt, 1)
            pe.wait_ge(s_joint_row, 1)
            pe.matmul(bank[1][:, 0:HIGH * LOW], ones[0:LOW * GT, :], hist_all[:, :, :].rearrange("p a b -> p (a b)"),
                      start=True, stop=True).then_inc(s_st, 1)
            pe.wait_ge(s_wtc, 1)

            def ranks(s, with_blocks):
                def step(r, j):
                    q = r * ROUND + j
                    view = bank[j % 2][:, 0:(K + 1) * NBX].rearrange("p (k n) -> p k n", n=NBX)
                    pe.wait_ge(s.hot, q + 1)
                    pe.wait_ge(s.base, q + 1)
                    wait(pe, s.prod, q - 1)
                    pe.matmul(view, ident[:, :], base[:, :].rearrange("p (a n) -> p a n", a=1).to_broadcast([P, K + 1, NBX]),
                              start=True, stop=False)
                    pe.matmul(view[:, 0:K, :], upper_b[:, :], hot[:, j % 2, :, :], start=False, stop=False)
                    for k in range(K):
                        last = pe.matmul(view[:, k + 1:K + 1, :], ones_b[:, :],
                                         hot[:, j % 2, k:k + 1, :].to_broadcast([P, K - k, NBX]),
                                         start=False, stop=(k == K - 1))
                    last.then_inc(s.rank, 1)
                    if with_blocks and j == 0:
                        pe.wait_ge(s_xld, 16 * (r + 1))
                        wait(pe, s_xTc, r)
                        pe.transpose(bank[2][:, 0:P], xb[:, :], ident[:, :]).then_inc(s_xT, 1)
                    if with_blocks and j == 1:
                        pe.wait_ge(s_xTc, r + 1)
                        wait(pe, s_aw, r)
                        pe.matmul(bank[3][:, 0:D], xbT[:, :], w1[:, 0, :], start=True, stop=True)
                        wait(pe, s_bw, r)
                        pe.matmul(bank[4][:, 0:D], xbT[:, :], w1[:, 1, :], start=True, stop=True).then_inc(s_ab, 1)
                run_steps(pe, NQ, 0, step)

            def turn_rows(s, c):
                pe.wait_ge(s.flt, 2 * (c + 1))
                if c:
                    pe.wait_ge(s.done, 2 * c)
                pe.transpose(bank[6][:, 0:P], list_f[:, 0, :], ident[:, :])
                pe.transpose(bank[6][:, P:2 * P], list_f[:, 1, :], ident[:, :]).then_inc(s.turn, 1)

            def complete_row(n):
                pe.wait_ge(s_done_by, n + 1)
                pe.matmul(bank[7][0:1, 0:P], done_by[:, n:n + 1], ident[:, :], start=True, stop=True).then_inc(s_done_row, 1)

            def turn_emb(s, layer, t):
                pe.wait_ge(s.emb, t + 1)
                wait(pe, s.turnc, t)
                area = bank[0][:, 2 * P:3 * P]
                if layer == 0:
                    pe.matmul(area, emb_x[:, :], ident[:, :], start=True, stop=False)
                    pe.matmul(area, emb_e[:, :], ident[:, :], start=False, stop=True).then_inc(s.turn, 1)
                else:
                    pe.transpose(area, emb_e[:, :], ident[:, :]).then_inc(s.turn, 1)

            def linear(s, layer, t):
                pe.wait_ge(s.turnc, t + 1)
                wait(pe, s.y, t)
                area = bank[4][:, LIN_AT:LIN_AT + D]
                pe.matmul(area, embT[:, :], (wl, wt)[layer][:, :], start=True, stop=False)
                pe.matmul(area, ones[0:1, :], (bl_bc, b_bc)[layer][0:1, :], start=False, stop=True).then_inc(s.lin, 1)

            def turn_step(s, layer, r, j):
                t = turn(r, 1)
                if t is not None and j == 2:
                    turn_emb(s, layer, t)
                if t is not None and j == 3:
                    linear(s, layer, t)

            def again(s, layer):
                def body(t, nb):
                    turn_emb(s, layer, t)
                    linear(s, layer, t)
                return body

            def in_bank4(s, layer, r, j):
                if j == 3:
                    turn_step(s, layer, r, 3)
                if j == 1 and turn(r, 2) is not None:
                    pe.wait_ge(s.y, turn(r, 2) + 1)

            def sums(s, r, j, lag, lhs, count, shared):
                at = back(r, j, lag, NG)
                if at is None:
                    if r > 0:
                        pe.wait_ge(s.acc, NPAIR)
                    shared()
                    return
                rr, jj, g = at
                pe.wait_ge(s.got[jj], slot_use(rr))
                for k in range(K):
                    h, i = k // (K // HALVES), k % (K // HALVES)
                    if i == 0:
                        wait(pe, s.acc, K * (g - 2) + (h + 1) * (K // HALVES))
                    if k == 0:
                        shared()
                    area = bank[4 + HALVES * (jj % 2) + h][:, i * SEG:(i + 1) * SEG]
                    last = pe.matmul(area[:, 0:D + 1], lhs(jj, k), got[:, jj, k, D:2 * D + 1], start=True, stop=True)
                    if count:
                        last = pe.matmul(area[:, D + 1:D + 2], hot_e[:, jj, k, :], ones_b[:, 0:1], start=True, stop=True)
                    if i == K // HALVES - 1:
                        last.then_inc(s.sum, 1)

            def edge0_step(r, j):
                at = back(r, j, 1, NG)
                if at is not None:
                    _, jj, g = at
                    pe.load(regs, blocks[0:1, span(g * K, K)])
                    nbs = [pe.snap(v, min_val=0, max_val=NB) for v in regs]
                    pe.wait_ge(edge0.turnc, g + 1)
                    wait(pe, edge0.hid, g - 1)
                    for k in range(K):
                        last = pe.matmul(bank[2 + jj % 2][:, k * D:(k + 1) * D], hot_n[:, jj % 2, k, :],
                                         a_tab[:, bass.ds(nbs[k] * D, D)], start=True, stop=True)
                    last.then_inc(edge0.a, 1)
                at = back(r, j, 0, NG)
                if at is not None:
                    g = at[2]
                    wait(pe, edge0.turnc, g - 1)
                if j == 2:
                    turn_step(node0, 0, r, 2)
                if at is not None:
                    pe.wait_ge(edge0.hot, g + 1)
                    for k in range(K):
                        last = pe.transpose(bank_b[j % 2][:, k * P:(k + 1) * P], hot_e[:, j, k, :], ident_b[:, :])
                    last.then_inc(edge0.turn, 1)
                at = back(r, j, 3, NG)
                if at is not None:
                    pe.wait_ge(edge0.whot, at[2] + 1)
                sums(edge0, r, j, 3, lambda jj, k: whot[:, jj % 2, k, :], True, lambda: in_bank4(node0, 0, r, j))

            def edge1_step(r, j):
                at = back(r, j, 1, NG)
                if at is not None:
                    pe.wait_ge(edge1.hot, at[2] + 1)
                sums(edge1, r, j, 1, lambda jj, k: whot[:, jj % 2, k, :], False, lambda: in_bank4(node1, 1, r, j))
                if j == 2:
                    turn_step(node1, 1, r, 2)

            pe.wait_ge(sort0.base, 1)
            ranks(sort0, True)
            pe.wait_ge(s_bel, 1)
            pe.wait_ge(s_aw, NB)
            pe.matmul(bank[3][:, 0:NBX], ones[:, :], below[:, :], start=True, stop=True).then_inc(s_st, 1)
            pe.wait_ge(s_bw, NB)
            complete_row(0)
            for c in range(NCH):
                turn_rows(pair0, c)
            pe.wait_ge(pair0.bld, 16)
            run_steps(pe, NG, EDGE_LAG, edge0_step)
            flag = pe.value_load(unsorted_i[0:1, 0:1], min_val=0, max_val=1)
            with pe.If(flag):
                ranks(sort1, False)
            complete_row(1)
            for c in range(NCH - TAIL_STEPS):
                turn_rows(pair1, c)
            for r in TURN_TAIL:
                for j in range(ROUND):
                    c = (r - TURN_TAIL[0]) * ROUND + j + NCH - TAIL_STEPS
                    if 0 <= c < NCH:
                        turn_rows(pair1, c)
                    turn_step(node0, 0, r, j)
            all_blocks_again(pe, 0, again(node0, 0))
            run_steps(pe, NG, EDGE_LAG, edge1_step)
            for r in TURN_TAIL:
                for j in range(ROUND):
                    turn_step(node1, 1, r, j)
            all_blocks_again(pe, 1, again(node1, 1))

        @block.vector
        def _(v):
            regs = [v.alloc_register(f"v_block{k}") for k in range(K)]
            turn_regs = [v.alloc_register("v_turn_block")]
            links = 0

            def link(ins):
                nonlocal links
                links += 1
                ins.then_inc(s_chain, 1)
                v.wait_ge(s_chain, links)

            for n in range(2):
                v.memset(edge[n][:, CW:NT], PAD_KEY).then_inc(s_pad, 1)
            v.memset(zeros[:, :], 0.0).then_inc(s_cv, 1)
            v.memset(ones[:, :], 1.0).then_inc(s_cv, 1)
            v.memset(ones_b[:, :], 1.0).then_inc(s_cv, 1)
            v.memset(got[:, :, :, 2 * D:2 * D + 1], 1.0)
            v.memset(start[0][:, 0:1], 0.0)
            link(v.memset(unsorted[:, :], 0.0))

            v.wait_ge(s_e[0], 32)
            v.tensor_scalar(digit_raw[0], edge[0][:, :], 10, None, ALU.arith_shift_right).then_inc(s_digit, 1)
            v.tensor_scalar(digit_raw[1], edge[0][:, :], 7, LOW - 1, ALU.arith_shift_right, ALU.bitwise_and).then_inc(s_digit, 1)
            link(v.tensor_scalar(other[:, 0:NT], edge[0][:, :], 7, None, ALU.arith_shift_right))
            link(v.tensor_copy(hi[0][:, :], other[:, 0:NT]))
            v.wait_ge(s_c, 7)
            v.tensor_copy(ident_b[:, :], ident[:, :]).then_inc(s_idb, 1)
            for half in range(2):
                part = slice(half * NT // 2, (half + 1) * NT // 2)
                v.wait_ge(s_key, 2)
                for d in range(LOW):
                    v.tensor_scalar(hot_low[:, half * NGT // 2:(half + 1) * NGT // 2, d, :],
                                    digit[1][:, part].rearrange("p (g t) -> p g t", t=GT), float(d), None, ALU.is_equal)
                for d in range(HIGH):
                    last = v.tensor_scalar(hot_high[:, d, part], digit[0][:, part], float(d), None, ALU.is_equal)
                last.then_inc(s_planes, 1)
            link(v.tensor_copy(digit_i[:, 0:1], pair_no[:, 0:1]))
            v.tensor_scalar(digit_i[:, 1:2], digit_i[:, 0:1], GT.bit_length() - 1, None, ALU.arith_shift_right)
            link(v.tensor_scalar(digit_i[:, 2:3], digit_i[:, 0:1], GT - 1, None, ALU.bitwise_and))
            link(v.tensor_copy(digit_f[:, :], digit_i[:, 1:3]))
            v.tensor_scalar(same_low[:, :], iota_f[:, 0:LOW], digit_f[:, 0:1], None, ALU.is_equal)
            link(v.tensor_scalar(same_tile[:, :], iota_f[:, 0:GT], digit_f[:, 1:2], None, ALU.is_equal))
            v.wait_ge(s_e[1], 80)
            link(v.tensor_scalar(other[:, 0:NT], edge[1][:, :], 7, None, ALU.arith_shift_right))
            link(v.tensor_copy(hi[1][:, :], other[:, 0:NT]))
            link(v.scalar_tensor_tensor(out=local[:, 0:CW], in0=shifted, scalar=0.0, in1=edge[1][:, 0:CW],
                                        op0=ALU.add, op1=ALU.is_lt, accum_out=unsorted[:, 0:1]))
            v.scalar_tensor_tensor(out=local[0:1, 0:REST - 1], in0=shift_tail[:, 1, 0:REST - 1], scalar=0.0,
                                   in1=shift_tail[:, 0, 0:REST - 1], op0=ALU.add, op1=ALU.is_lt,
                                   accum_out=unsorted[0:1, 1:2]).then_inc(s_flag0, 1)
            for f in range(2):
                v.tensor_copy(stage[:, :, f], edge[f][:, :]).then_inc(s_copy1, 1)
            v.wait_ge(s_joint, 1)
            rows = LOW * GT
            link(v.tensor_tensor(hist_prod[:, :, :], bank[0][0:rows, 0:HIGH * GT].rearrange("p (a t) -> p a t", t=GT),
                                 same_tile[0:rows, :].rearrange("p (o t) -> p o t", o=1).to_broadcast([rows, HIGH, GT]),
                                 ALU.mult))
            link(v.tensor_reduce(hist_high[:, :], hist_prod[:, :, :], AX_X, ALU.add))
            v.tensor_tensor(hist_all[:, :, :],
                            hist_high[:, :].rearrange("p (a o) -> p a o", o=1).to_broadcast([rows, HIGH, LOW]),
                            same_low[0:rows, :].rearrange("p (o b) -> p o b", o=1).to_broadcast([rows, HIGH, LOW]),
                            ALU.mult).then_inc(s_joint_row, 1)
            v.wait_ge(s_st, 1)
            link(v.tensor_reduce(unsorted[:, 0:1], bank[7][:, 0:2], AX_X, ALU.add))
            v.wait_ge(s_st, 2)
            link(v.tensor_copy(pick[:, :], bank[1][:, 0:NBX]))
            link(v.tensor_tensor_scan(start[0][:, 1:NBX + 1], pick[:, :], zeros[:, 0:NBX], 0.0, ALU.add, ALU.add))
            v.tensor_copy(base[:, :], start[0][:, 0:NBX]).then_inc(sort0.base, 1)
            v.wait_ge(s_wt, 1)
            v.tensor_copy(wt[:, :], bank[2][:, 0:P]).then_inc(s_wtc, 1)

            def sort_extras():
                v.tensor_scalar(unsorted_i[:, :], unsorted[0:1, 0:1], 1.0, None, ALU.min).then_inc(s_flag, 1)
                v.tensor_copy(keyf, edge[1][:, :])
                v.memset(a_tab[:, NB * D:NBX * D], 0.0)
                v.wait_ge(s_w, 16 * 8)

            def count(nb):
                return v.tensor_scalar(unused, keyf, bound_f[:, span(nb, 1)], None, ALU.is_lt, ALU.add,
                                       accum_out=below[:, span(nb, 1)])

            def places(s, n, with_blocks, head=2, hook=None):
                def step(r, j):
                    at = back(r, j, 0, NQ)
                    if at is not None:
                        q = at[2]
                        wait(v, s.rank, q - 1)
                        wait(v, s.prod, q - 1)
                        v.tensor_tensor(hot[:, j % 2, :, :],
                                        hi[n][:, span(q * K, K)].rearrange("p (k a) -> p k a", a=1).to_broadcast([P, K, NBX]),
                                        iota_b[:, 0:NBX].rearrange("p (a n) -> p a n", a=1).to_broadcast([P, K, NBX]),
                                        ALU.is_equal).then_inc(s.hot, 1)
                    at = back(r, j, 1, NQ)
                    if at is not None:
                        rr, jj, q = at
                        v.wait_ge(s.base, q + 2)
                        wait(v, s.pos, q)
                        v.tensor_tensor(rank_prod[:, :, :], hot[:, jj % 2, :, :],
                                        bank[jj % 2][:, 0:K * NBX].rearrange("p (k n) -> p k n", n=NBX),
                                        ALU.mult).then_inc(s.prod, 1)
                        if with_blocks and j == 2:
                            v.wait_ge(s_ab, r + 1)
                            v.tensor_tensor(a_tab[:, span(r * D, D)], bank[3][:, 0:D], b1_bc[:, :], ALU.add).then_inc(s_aw, 1)
                        if with_blocks and j == 3:
                            wait(v, s_cnt1, r)
                            count(r).then_inc(s_cnt1, 1)
                        if with_blocks and isinstance(r, int) and (r, j) == (0, 1):
                            sort_extras()
                        v.wait_ge(s.prod, q + 1)
                        if not (isinstance(rr, int) and rr < 1):
                            v.wait_ge(s.wrote[jj], slot_use(rr - 1))
                        with nc.allow_low_precision(reason="places are whole numbers below 2 ** 24"):
                            v.tensor_reduce(pos[:, jj, :], rank_prod[:, :, :], AX_X, ALU.add).then_inc(s.pos, 1)
                    if hook is not None and isinstance(r, int):
                        hook(r * ROUND + j)
                run_steps(v, NQ, SORT_LAG, step, head=head)

            PAIR_PARTS = NCH + 3

            def pairs(s, n, part):
                st = start[n]
                if part == 0:
                    link(v.tensor_copy(start_i[:, 0:NBX], st[:, 0:NBX]))
                    link(v.tensor_scalar(first_i[:, 0:NBX], start_i[:, 0:NBX], 7, None, ALU.arith_shift_right))
                    link(v.tensor_copy(first_f[:, 0:NBX], first_i[:, 0:NBX]))
                    link(v.tensor_scalar(start_i[:, 0:NB], st[:, 1:NBX], -1.0, None, ALU.add))
                    link(v.tensor_scalar(last_i[:, 0:NB], start_i[:, 0:NB], 7, None, ALU.arith_shift_right))
                    link(v.tensor_copy(last_f[:, 0:NB], last_i[:, 0:NB]))
                elif part == 1:
                    link(v.tensor_tensor(last_f[:, 0:NB], last_f[:, 0:NB], first_f[:, 0:NB], ALU.subtract))
                    link(v.tensor_tensor(pick[:, 0:NB], st[:, 1:NBX], st[:, 0:NB], ALU.is_gt))
                    link(v.scalar_tensor_tensor(out=npair[:, :], in0=last_f[:, 0:NB], scalar=1.0, in1=pick[:, 0:NB],
                                                op0=ALU.add, op1=ALU.mult))
                    link(v.tensor_tensor_scan(pair_end[:, :], npair[:, :], zeros[:, 0:NB], 0.0, ALU.add, ALU.add))
                    link(v.memset(shift_f[:, :], -4.0 * NPAIR))
                    link(v.tensor_tensor(shift_f[:, 0:NB], first_f[:, 0:NB], pair_end[:, :], ALU.subtract))
                    link(v.tensor_tensor(shift_f[:, 0:NB], shift_f[:, 0:NB], npair[:, :], ALU.add))
                elif part < PAIR_PARTS - 1:
                    c = part - 2
                    link(v.tensor_scalar(pick[:, 0:NB], pair_end[:, :], pair_no[:, c:c + 1], None, ALU.is_le, ALU.add,
                                         accum_out=pair_block[:, c:c + 1]))
                    link(v.scalar_tensor_tensor(out=pick[:, :], in0=iota_f[:, 0:NBX], scalar=pair_block[:, c:c + 1],
                                                in1=shift_f[:, :], op0=ALU.is_equal, op1=ALU.mult,
                                                accum_out=pair_row[:, c:c + 1]))
                else:
                    link(v.tensor_tensor(pair_row[:, :], pair_row[:, :], pair_no[:, :], ALU.add))
                    link(v.tensor_scalar(pair_row[:, :], pair_row[:, :], 0.0, REAL_ROWS - 1.0, ALU.max, ALU.min))
                    v.tensor_scalar(pick[:, 0:NB - 1], pair_end[:, 0:NB - 1], turn_no[:, n:n + 1], None, ALU.is_le, ALU.add,
                                    accum_out=done_by[:, n:n + 1]).then_inc(s_done_by, 1)
                    v.tensor_copy(pair_row_i[n][:, :], pair_row[:, :])
                    v.tensor_scalar(pair_lo[n][:, :], pair_block[:, :], float(P), None, ALU.mult)
                    v.tensor_copy(pair_block_i[n][:, :], pair_block[:, :]).then_inc(s.calc, 1)
                    v.wait_ge(s.calc, 1)

            def turns(n):
                v.wait_ge(s_done_row, n + 1)
                link(v.tensor_scalar(turn_f[:, :], bank[7][0:1, 0:TURNS - 1], -1.0, None, ALU.add))
                link(v.tensor_tensor_scan(turn_f[:, :], ones[0:1, 0:TURNS - 1], turn_f[:, :], -1.0, ALU.add, ALU.min))
                link(v.tensor_scalar(turn_skip[:, :], turn_f[:, :], 0.0, NB + 1.0, ALU.is_lt, ALU.mult))
                v.tensor_tensor(turn_block[n][:, :], turn_f[:, :], turn_skip[:, :], ALU.add)
                v.tensor_scalar(turn_store[n][:, :], turn_f[:, :], 0.0, None, ALU.max)
                v.tensor_scalar(late[:, n:n + 1], turn_f[:, TURNS - 2:TURNS - 1], NB - 2.0, None, ALU.is_lt).then_inc(s_turns, 1)

            def rows_float(s, n, c):
                v.wait_ge(s.got[c % 2], 16 * (c // 2 + 1))
                if c:
                    v.wait_ge(s.turn, c)
                v.tensor_scalar(list_f[:, 0, :], list_row[:, c % 2, :, n], pair_lo[n][:, c:c + 1], None,
                                ALU.subtract).then_inc(s.flt, 1)
                v.tensor_copy(list_f[:, 1, :], list_row[:, c % 2, :, 1 - n]).then_inc(s.flt, 1)

            def one_hots(s, r, j, out, free):
                at = back(r, j, 0, NG)
                if at is not None:
                    g = at[2]
                    wait(v, s.sum, HALVES * (g - free + 1))
                    for k in range(K):
                        last = v.tensor_scalar(out(k), iota_b[:, :], local[:, span(g * K + k, 1)], None, ALU.is_equal)
                    last.then_inc(s.hot, 1)

            def add_sums(s, r, j, lag, cols, between, leave):
                at = back(r, j, lag, NG)
                if at is not None:
                    g = at[2]
                    v.load(regs, blocks[0:1, span(g * K, K)])
                    nbs = [v.snap(x_, min_val=0, max_val=NB) for x_ in regs]
                for k in range(K):
                    h, i = k // (K // HALVES), k % (K // HALVES)
                    if k == 0:
                        leave(k)
                    if between is not None:
                        between(k)
                    if at is not None:
                        v.wait_ge(s.sum, HALVES * g + h + 1)
                    if k:
                        leave(k)
                    if at is not None:
                        wait(v, s.acc, K * g + k)
                        here = acc[:, bass.ds(nbs[k] * SEG, cols)]
                        v.tensor_tensor(here, here, bank[4 + HALVES * (at[1] % 2) + h][:, i * SEG:i * SEG + cols],
                                        ALU.add).then_inc(s.acc, 1)

            def sum_inverse(s, layer, t, nb, i):
                seg = acc[:, span(nb * SEG + D, 1)]
                if i == 0:
                    wait(v, s.inv, t)
                    if layer == 0:
                        v.tensor_scalar(seg_w[:, :], seg, 1e-9, 2.0, ALU.add, ALU.mult).then_inc(s.seg, 1)
                    else:
                        v.tensor_scalar(seg_w[:, :], seg, 1.0, None, ALU.max).then_inc(s.seg, 1)
                if i == 1:
                    v.wait_ge(s.seg, t + 1)
                    wait(v, s.emb, t)
                    v.reciprocal(seg_inv[:, :], seg_w[:, :]).then_inc(s.inv, 1)

            def residual(s, layer, t):
                v.wait_ge(s.lin, t + 1)
                v.wait_ge(s.xres, 16 * (t + 1))
                wait(v, s.res, t)
                if layer == 0:
                    v.scalar_tensor_tensor(out=y[:, :], in0=bank[4][:, LIN_AT:LIN_AT + D], scalar=0.0, in1=x_res[:, :],
                                           op0=ALU.max, op1=ALU.add).then_inc(s.y, 1)
                else:
                    v.tensor_tensor(y[:, :], bank[4][:, LIN_AT:LIN_AT + D], x_res[:, :], ALU.add).then_inc(s.y, 1)

            def statistics(s, t):
                v.wait_ge(s.y, t + 1)
                wait(v, s.mv, t)
                v.bn_stats(stats[:, :], y[:, :]).then_inc(s.st, 1)

            def aggregate(s, t):
                v.wait_ge(s.st, t + 1)
                wait(v, s.shift, t)
                v.sem_inc(s.go, 1)
                v.bn_aggr(mv[:, :], stats[:, :]).then_inc(s.mv, 1)

            ROOT_STEPS = 9
            ROOT_FACTOR = [1.0]
            for _ in range(3):
                ROOT_FACTOR.append(-2.0 * ROOT_FACTOR[-1] ** 3)

            def root_step(s, t, i):
                v.wait_ge(s.root, t * ROOT_STEPS + i) if i else v.wait_ge(s.mv, t + 1)
                if i == 0:
                    wait(v, s.root, t * ROOT_STEPS)
                    ins = v.tensor_scalar(var_eps[:, :], mv[:, 1:2], EPS, None, ALU.add)
                elif i == 1:
                    ins = v.tensor_scalar(half_bits[:, :], var_eps[:, :].bitcast(I32), 1, None, ALU.arith_shift_right)
                elif i == 2:
                    wait(v, s.shift, t)
                    ins = v.tensor_scalar(root[:, :].bitcast(I32), half_bits[:, :], -1.0, float(0x5F3759DF), ALU.mult, ALU.add)
                elif i % 2:
                    ins = v.scalar_tensor_tensor(out=root_sq[:, :], in0=root[:, :], scalar=var_eps[:, :], in1=root[:, :],
                                                 op0=ALU.mult, op1=ALU.mult)
                else:
                    ins = v.scalar_tensor_tensor(out=root[:, :], in0=root_sq[:, :], scalar=-3.0 * ROOT_FACTOR[i // 2 - 2] ** 2,
                                                 in1=root[:, :], op0=ALU.add, op1=ALU.mult)
                ins.then_inc(s.root, 1)

            def mean_shift(s, t):
                v.wait_ge(s.root, (t + 1) * ROOT_STEPS)
                wait(v, s.res, t)
                f = 1.0 / ROOT_FACTOR[-1]
                v.tensor_scalar(rstd[:, :], root[:, :], f, None, ALU.mult)
                v.scalar_tensor_tensor(out=shift[:, :], in0=mv[:, 0:1], scalar=-f, in1=root[:, :],
                                       op0=ALU.mult, op1=ALU.mult).then_inc(s.shift, 1)

            turn_nb = [None]

            def turn_begin(s, es, layer, r, j):
                t = turn(r, 1)
                if t is not None and j == 0:
                    turn_nb[0] = turn_is(v, turn_regs, turn_block[layer], t)

            def turn_step(s, es, layer, r, j, k):
                t = turn(r, 2)
                if t is not None and (j, k) == (0, 1):
                    residual(s, layer, t)
                if t is not None and (j, k) == (1, 0):
                    statistics(s, t)
                if t is not None and (j, k) == (1, 1):
                    aggregate(s, t)
                if t is not None and 0 <= j * K + k - K - 2 < ROOT_STEPS:
                    root_step(s, t, j * K + k - K - 2)
                if t is not None and (j, k) == (3, 3):
                    mean_shift(s, t)
                t = turn(r, 1)
                if t is not None and j == 0 and k in (1, 2):
                    if k == 1:
                        added = r * ROUND * K - (4, 2)[layer] * K
                        wait(v, es.acc, min(added, NPAIR) if isinstance(r, int) else added)
                    sum_inverse(s, layer, t, turn_nb[0], k - 1)
                if t is not None and (j, k) == (2, 0):
                    v.wait_ge(s.emb, t + 1)

            def again(s, layer):
                def body(t, nb):
                    for i in range(2):
                        sum_inverse(s, layer, t, nb, i)
                    residual(s, layer, t)
                    statistics(s, t)
                    aggregate(s, t)
                    for i in range(ROOT_STEPS):
                        root_step(s, t, i)
                    mean_shift(s, t)
                return body

            def edge0_step(r, j):
                turn_begin(node0, edge0, 0, r, j)
                one_hots(edge0, r, j, lambda k: hot_e[:, j, k, :], ROUND)
                at = back(r, j, 2, NG)
                if at is not None:
                    rr, jj, g = at
                    v.wait_ge(edge0.a, g + 1)
                    v.wait_ge(edge0.got[jj], slot_use(rr))
                    wait(v, edge0.logit, g - 1)
                    v.tensor_tensor(hidden[:, jj % 2, :, :],
                                    bank[2 + jj % 2][:, :].rearrange("p (k d) -> p k d", d=D),
                                    got[:, jj, :, 0:D], ALU.add).then_inc(edge0.hid, 1)
                    wait(v, edge0.weight, g - 1)

                def logits(k):
                    if at is not None:
                        if k == 0:
                            v.wait_ge(edge0.hid, at[2] + 1)
                        h = hidden[:, at[1] % 2, k, :]
                        ins = v.scalar_tensor_tensor(out=h, in0=h, scalar=0.0, in1=w2[:, :], op0=ALU.max, op1=ALU.mult,
                                                     accum_out=logit[:, at[1] % 2, k:k + 1])
                        if k == K - 1:
                            ins.then_inc(edge0.logit, 1)

                add_sums(edge0, r, j, 4, SEG, logits, lambda k: turn_step(node0, edge0, 0, r, j, k))

            def edge1_step(r, j):
                turn_begin(node1, edge1, 1, r, j)
                one_hots(edge1, r, j, lambda k: whot[:, j % 2, k, :], 2)
                add_sums(edge1, r, j, 2, D + 1, None, lambda k: turn_step(node1, edge1, 1, r, j, k))

            CLEAR = range(2 * NT, NBX * SEG, NT)

            def beside_sort(q):
                part = q - 2
                if 0 <= part < PAIR_PARTS:
                    pairs(pair0, 0, part)
                elif 0 <= part - PAIR_PARTS < len(CLEAR):
                    at = CLEAR[part - PAIR_PARTS]
                    v.wait_ge(s_list1, 32)
                    link(v.memset(acc[:, at:min(at + NT, NBX * SEG)], 0.0))

            places(sort0, 0, True, -(-(2 + PAIR_PARTS + len(CLEAR)) // ROUND), beside_sort)
            v.wait_ge(s_cnt1, NB)
            count(NB).then_inc(s_bel, 1)
            v.wait_ge(s_st, 3)
            link(v.tensor_copy(start[1][:, 0:NBX], bank[3][:, 0:NBX]))
            for c in range(NCH):
                rows_float(pair0, 0, c)
                pairs(pair1, 1, c)
            turns(0)
            v.wait_ge(s_bel, 1)
            link(v.memset(acc[:, 0:2 * NT], 0.0))
            v.wait_ge(pair0.bld, 16)
            v.wait_ge(pair0.done, 2 * NCH)
            for part in range(NCH, PAIR_PARTS):
                pairs(pair1, 1, part)
            run_steps(v, NG, EDGE_LAG, edge0_step)

            flag = v.value_load(unsorted_i[0:1, 0:1], min_val=0, max_val=1)
            with v.If(flag):
                for j in range(ROUND):
                    v.wait_ge(sort0.wrote[j], slot_use(ROUNDS_SORT - 1))
                v.wait_ge(sort0.base, NQ + 1)
                v.tensor_copy(base[:, :], start[1][:, 0:NBX]).then_inc(sort1.base, 1)
                places(sort1, 1, False)
            v.wait_ge(edge0.acc, NPAIR)
            for c in range(NCH - TAIL_STEPS):
                rows_float(pair1, 1, c)
            for r in TURN_TAIL:
                for j in range(ROUND):
                    c = (r - TURN_TAIL[0]) * ROUND + j + NCH - TAIL_STEPS
                    if 0 <= c < NCH:
                        rows_float(pair1, 1, c)
                    turn_begin(node0, edge0, 0, r, j)
                    for k in range(K):
                        turn_step(node0, edge0, 0, r, j, k)
            turns(1)
            all_blocks_again(v, 0, again(node0, 0))
            v.wait_ge(node0.res, TURNS)
            link(v.memset(acc[:, :], 0.0))
            v.wait_ge(pair1.done, 2 * NCH)
            v.wait_ge(pair1.bld, 16)
            run_steps(v, NG, EDGE_LAG, edge1_step)
            v.wait_ge(edge1.acc, NPAIR)
            for r in TURN_TAIL:
                for j in range(ROUND):
                    turn_begin(node1, edge1, 1, r, j)
                    for k in range(K):
                        turn_step(node1, edge1, 1, r, j, k)
            all_blocks_again(v, 1, again(node1, 1))


_INS = ["x", "src", "dst", "L0_gnn_W1", "L0_gnn_b1", "L0_gnn_W2", "L0_gnn_b2", "L0_gnn_Wl", "L0_gnn_bl", "L1_gnn_W", "L1_gnn_b"]


def kernel(**inputs):
    import numpy as _np
    import concourse.bacc as _bacc
    from concourse import mybir as _mybir
    from concourse.bass_utils import run_bass_kernel_spmd as _run

    nc = _bacc.Bacc("TRN2", target_bir_lowering=False, num_devices=1)
    arrays, args = {}, []
    for name in _INS:
        a = _np.ascontiguousarray(inputs[name])
        arrays[f"in_{name}_dram"] = a
        args.append(nc.dram_tensor(f"in_{name}_dram", a.shape, _mybir.dt.from_np(a.dtype), kind="ExternalInput").ap())
    out = nc.dram_tensor("out_0_dram", (N, D), _mybir.dt.float32, kind="ExternalOutput").ap()
    build(nc, *args, out)
    r = _run(nc, [arrays], core_ids=[0])
    return r.results[0]["out_0_dram"]
```
